# Optimizing a Trainium2 kernel written in Bass

```python
import numpy as np
import jax
import jax.numpy as jnp

def _softmax(x, axis=-1):
    return jax.nn.softmax(x, axis=axis)

def _gelu(x):
    return jax.nn.gelu(x, approximate=True)

def _silu(x):
    return jax.nn.silu(x)

def _sigmoid(x):
    return jax.nn.sigmoid(x)

def _layernorm(x, axis=-1, eps=1e-05):
    m = jnp.mean(x, axis=axis, keepdims=True)
    v = jnp.var(x, axis=axis, keepdims=True)
    return (x - m) / jnp.sqrt(v + eps)

def _scatter_add(tgt, idx, src, axis=0):
    return tgt.at[idx].add(src)

def _segment_sum(src, seg, n):
    return jax.ops.segment_sum(src, seg, n)
kernel_name = 'mk_adj_preln_d1_adj_r2_35d757'

def setup_inputs(seed: int=0):
    np.random.seed(seed)
    _w = jnp.asarray

    def _rec_inputs():
        import jax
        import jax.numpy as jnp
        _gk = jax.random.key(seed)
        x = 1.444e-06 + 0.02 * jax.random.normal(jax.random.fold_in(_gk, 1), (64, 128, 512), jnp.float32)
        _w = (1.0 + jnp.arange(128, dtype=jnp.float32)) ** (-0.5)
        _w = _w / _w.mean()
        _pij = jnp.clip(0.03125 * _w[:, None] * _w[None, :], 0.0, 1.0)
        _a = jax.random.uniform(jax.random.fold_in(_gk, 2), (64, 128, 128)) < _pij
        _a = jnp.logical_or(_a, jnp.eye(128, dtype=bool))
        _af = _a.astype(jnp.float32)
        adj = _af
        return (x, adj)
    x, adj = _rec_inputs()

    def _L0_gnn_setup():
        import jax, jax.numpy as jnp
        import numpy as np
        B, N, D, H = (4, 1024, 512, 8)
        HD = D // H
        SCALE = HD ** (-0.5)
        LN_EPS = 1e-05

        def _lin(x, w, b):
            return x @ w.T + b

        def _ln(x, g, b):
            m = x.mean(-1, keepdims=True)
            v = ((x - m) ** 2).mean(-1, keepdims=True)
            return (x - m) / jnp.sqrt(v + LN_EPS) * g + b

        def _attn(q, k, v, mask):
            Bq, Nt, _ = q.shape
            Ns = k.shape[1]
            qh = q.reshape(Bq, Nt, H, HD).transpose(0, 2, 1, 3)
            kh = k.reshape(Bq, Ns, H, HD).transpose(0, 2, 1, 3)
            vh = v.reshape(Bq, Ns, H, HD).transpose(0, 2, 1, 3)
            scores = jnp.einsum('bhid,bhjd->bhij', qh, kh) * SCALE
            scores = jnp.where(mask[:, None] > 0, scores, -jnp.inf)
            w = jax.nn.softmax(scores, axis=-1)
            out = jnp.einsum('bhij,bhjd->bhid', w, vh)
            return out.transpose(0, 2, 1, 3).reshape(Bq, Nt, D)
        key = jax.random.key(seed)
        ks = jax.random.split(key, 16)
        pe = jax.random.normal(ks[0], (B, N, D), jnp.float32) * 0.02
        inc = jax.random.randint(ks[1], (B, N, N), 0, 2).astype(jnp.float32)
        inc = jnp.maximum(inc, jnp.eye(N, dtype=jnp.float32)[None])

        def w(k, o, i):
            return jax.random.normal(k, (o, i), jnp.float32) / np.sqrt(i)
        inp = {'prompt_embeddings': pe, 'incidence_matrix': inc, 'n2e_q_w': w(ks[2], D, D), 'n2e_q_b': jnp.zeros((D,), jnp.float32), 'n2e_k_w': w(ks[3], D, D), 'n2e_k_b': jnp.zeros((D,), jnp.float32), 'n2e_v_w': w(ks[4], D, D), 'n2e_v_b': jnp.zeros((D,), jnp.float32), 'e2n_q_w': w(ks[5], D, D), 'e2n_q_b': jnp.zeros((D,), jnp.float32), 'e2n_k_w': w(ks[6], D, D), 'e2n_k_b': jnp.zeros((D,), jnp.float32), 'e2n_v_w': w(ks[7], D, D), 'e2n_v_b': jnp.zeros((D,), jnp.float32), 'norm1_g': jnp.ones((D,), jnp.float32), 'norm1_b': jnp.zeros((D,), jnp.float32), 'norm2_g': jnp.ones((D,), jnp.float32), 'norm2_b': jnp.zeros((D,), jnp.float32), 'norm3_g': jnp.ones((D,), jnp.float32), 'norm3_b': jnp.zeros((D,), jnp.float32), 'ffn_w1': w(ks[8], 4 * D, D), 'ffn_b1': jnp.zeros((4 * D,), jnp.float32), 'ffn_w2': w(ks[9], D, 4 * D), 'ffn_b2': jnp.zeros((D,), jnp.float32)}
        return inp
    _L0_gnn_all = _L0_gnn_setup()
    _L0_gnn_in = {k: v for k, v in _L0_gnn_all.items() if k in ('n2e_q_w', 'n2e_q_b', 'n2e_k_w', 'n2e_k_b', 'n2e_v_w', 'n2e_v_b', 'e2n_q_w', 'e2n_q_b', 'e2n_k_w', 'e2n_k_b', 'e2n_v_w', 'e2n_v_b', 'norm1_g', 'norm1_b', 'norm2_g', 'norm2_b', 'norm3_g', 'norm3_b', 'ffn_w1', 'ffn_b1', 'ffn_w2', 'ffn_b2')}
    del _L0_gnn_all
    return {'x': x, 'adj': adj, 'L0_gnn_n2e_q_w': _L0_gnn_in['n2e_q_w'], 'L0_gnn_n2e_q_b': _L0_gnn_in['n2e_q_b'], 'L0_gnn_n2e_k_w': _L0_gnn_in['n2e_k_w'], 'L0_gnn_n2e_k_b': _L0_gnn_in['n2e_k_b'], 'L0_gnn_n2e_v_w': _L0_gnn_in['n2e_v_w'], 'L0_gnn_n2e_v_b': _L0_gnn_in['n2e_v_b'], 'L0_gnn_e2n_q_w': _L0_gnn_in['e2n_q_w'], 'L0_gnn_e2n_q_b': _L0_gnn_in['e2n_q_b'], 'L0_gnn_e2n_k_w': _L0_gnn_in['e2n_k_w'], 'L0_gnn_e2n_k_b': _L0_gnn_in['e2n_k_b'], 'L0_gnn_e2n_v_w': _L0_gnn_in['e2n_v_w'], 'L0_gnn_e2n_v_b': _L0_gnn_in['e2n_v_b'], 'L0_gnn_norm1_g': _L0_gnn_in['norm1_g'], 'L0_gnn_norm1_b': _L0_gnn_in['norm1_b'], 'L0_gnn_norm2_g': _L0_gnn_in['norm2_g'], 'L0_gnn_norm2_b': _L0_gnn_in['norm2_b'], 'L0_gnn_norm3_g': _L0_gnn_in['norm3_g'], 'L0_gnn_norm3_b': _L0_gnn_in['norm3_b'], 'L0_gnn_ffn_w1': _L0_gnn_in['ffn_w1'], 'L0_gnn_ffn_b1': _L0_gnn_in['ffn_b1'], 'L0_gnn_ffn_w2': _L0_gnn_in['ffn_w2'], 'L0_gnn_ffn_b2': _L0_gnn_in['ffn_b2']}

def reference(x, adj, L0_gnn_n2e_q_w, L0_gnn_n2e_q_b, L0_gnn_n2e_k_w, L0_gnn_n2e_k_b, L0_gnn_n2e_v_w, L0_gnn_n2e_v_b, L0_gnn_e2n_q_w, L0_gnn_e2n_q_b, L0_gnn_e2n_k_w, L0_gnn_e2n_k_b, L0_gnn_e2n_v_w, L0_gnn_e2n_v_b, L0_gnn_norm1_g, L0_gnn_norm1_b, L0_gnn_norm2_g, L0_gnn_norm2_b, L0_gnn_norm3_g, L0_gnn_norm3_b, L0_gnn_ffn_w1, L0_gnn_ffn_b1, L0_gnn_ffn_w2, L0_gnn_ffn_b2):
    import jax
    import jax.numpy as jnp

    def _L0_gnn_ref(prompt_embeddings, incidence_matrix, n2e_q_w, n2e_q_b, n2e_k_w, n2e_k_b, n2e_v_w, n2e_v_b, e2n_q_w, e2n_q_b, e2n_k_w, e2n_k_b, e2n_v_w, e2n_v_b, norm1_g, norm1_b, norm2_g, norm2_b, norm3_g, norm3_b, ffn_w1, ffn_b1, ffn_w2, ffn_b2):
        import jax, jax.numpy as jnp
        import numpy as np
        B, N, D, H = (4, 1024, 512, 8)
        HD = D // H
        SCALE = HD ** (-0.5)
        LN_EPS = 1e-05

        def _lin(x, w, b):
            return x @ w.T + b

        def _ln(x, g, b):
            m = x.mean(-1, keepdims=True)
            v = ((x - m) ** 2).mean(-1, keepdims=True)
            return (x - m) / jnp.sqrt(v + LN_EPS) * g + b

        def _attn(q, k, v, mask):
            Bq, Nt, _ = q.shape
            Ns = k.shape[1]
            qh = q.reshape(Bq, Nt, H, HD).transpose(0, 2, 1, 3)
            kh = k.reshape(Bq, Ns, H, HD).transpose(0, 2, 1, 3)
            vh = v.reshape(Bq, Ns, H, HD).transpose(0, 2, 1, 3)
            scores = jnp.einsum('bhid,bhjd->bhij', qh, kh) * SCALE
            scores = jnp.where(mask[:, None] > 0, scores, -jnp.inf)
            w = jax.nn.softmax(scores, axis=-1)
            out = jnp.einsum('bhij,bhjd->bhid', w, vh)
            return out.transpose(0, 2, 1, 3).reshape(Bq, Nt, D)
        pe = prompt_embeddings
        n2e_mask = incidence_matrix.transpose(0, 2, 1)
        eq = _lin(pe, n2e_q_w, n2e_q_b)
        nk = _lin(pe, n2e_k_w, n2e_k_b)
        nv = _lin(pe, n2e_v_w, n2e_v_b)
        edge_features = _attn(eq, nk, nv, n2e_mask)
        edge_features = _ln(edge_features + pe, norm1_g, norm1_b)
        nq = _lin(pe, e2n_q_w, e2n_q_b)
        ek = _lin(edge_features, e2n_k_w, e2n_k_b)
        ev = _lin(edge_features, e2n_v_w, e2n_v_b)
        node_updates = _attn(nq, ek, ev, incidence_matrix)
        node_features = _ln(pe + node_updates, norm2_g, norm2_b)
        h = jax.nn.gelu(_lin(node_features, ffn_w1, ffn_b1), approximate=False)
        out = _ln(node_features + _lin(h, ffn_w2, ffn_b2), norm3_g, norm3_b)
        return out
    h = jnp.maximum(_layernorm(x, axis=-1), 0.0)
    x = x + _L0_gnn_ref(h, adj, L0_gnn_n2e_q_w, L0_gnn_n2e_q_b, L0_gnn_n2e_k_w, L0_gnn_n2e_k_b, L0_gnn_n2e_v_w, L0_gnn_n2e_v_b, L0_gnn_e2n_q_w, L0_gnn_e2n_q_b, L0_gnn_e2n_k_w, L0_gnn_e2n_k_b, L0_gnn_e2n_v_w, L0_gnn_e2n_v_b, L0_gnn_norm1_g, L0_gnn_norm1_b, L0_gnn_norm2_g, L0_gnn_norm2_b, L0_gnn_norm3_g, L0_gnn_norm3_b, L0_gnn_ffn_w1, L0_gnn_ffn_b1, L0_gnn_ffn_w2, L0_gnn_ffn_b2)
    return x

_drawn_inputs = setup_inputs


def setup_inputs(seed=0):
    import zlib

    import numpy as np

    out = dict(_drawn_inputs(seed))
    spreads = {'L0_gnn_n2e_q_b': (0.0, 0.597),
     'L0_gnn_n2e_k_b': (0.0, 0.8),
     'L0_gnn_n2e_v_b': (0.0, 0.1),
     'L0_gnn_e2n_q_b': (0.0, 0.1),
     'L0_gnn_e2n_k_b': (0.0, 0.8),
     'L0_gnn_e2n_v_b': (0.0, 0.1),
     'L0_gnn_norm1_g': (1.0, 0.2),
     'L0_gnn_norm1_b': (0.0, 0.1),
     'L0_gnn_norm2_g': (1.0, 0.2),
     'L0_gnn_norm2_b': (0.0, 0.1),
     'L0_gnn_norm3_g': (1.0, 0.2),
     'L0_gnn_norm3_b': (0.0, 0.1),
     'L0_gnn_ffn_b1': (0.0, 0.1),
     'L0_gnn_ffn_b2': (0.0, 0.1)}
    factors = {}
    for name, (base, spread) in spreads.items():
        noise = np.random.default_rng([zlib.crc32(name.encode()), seed]).standard_normal(out[name].shape)
        drawn = base * np.exp(spread * noise) if base else spread * noise
        out[name] = jnp.asarray(drawn.astype(out[name].dtype))
    for name, factor in factors.items():
        out[name] = (out[name] * factor).astype(out[name].dtype)
    return out
```

```python
from contextlib import ExitStack

import concourse.bass as bass
from concourse import mybir

F32 = mybir.dt.float32
F32R = mybir.dt.float32r
BF16 = mybir.dt.bfloat16
ALU = mybir.AluOpType
ACT = mybir.ActivationFunctionType
AX = mybir.AxisListType

P = 128
D = 512
KT = D // P
H = 8
HD = D // H
HU = H // 2
HV = HD + 1
GB = 4
R = GB * P
DF = 2048
FT = DF // P
LN_EPS = 1e-5
SCALE = HD ** -0.5
MASKED = -1e30

UNITS = 4 * GB
TILES = 24
PRO_TILES = 12
TILE_KIND = ([("q2", m) for m in range(KT)] + [("ev", 0), ("ev", 1), ("ev", 2)]
             + [("ek", m) for m in range(KT)] + [("ev", 3)]
             + [(w, m) for m in range(KT) for w in ("q", "k")] + [("v", b) for b in range(GB)])
TILE_OF = {k: t for t, k in enumerate(TILE_KIND)}
TRANSPOSES = 8


def steps_of_group(first, last):
    halves = [("half", t, s) for t in range(TILES) for s in range(2)]
    out = []

    def tile(kind, idx, parts=(0, 1)):
        for s in parts:
            out.append(("half", TILE_OF[(kind, idx)], s))
            if s == 1:
                out.append(("evac", TILE_OF[(kind, idx)]))

    def finish(u):
        out.extend([("pt", u), ("pt_evac", u)])

    def values(u):
        out.extend([("av", u), ("norm", u), ("add_h", u)])

    for u in range(UNITS):
        layer, v = divmod(u, 8)
        b = v // 2
        out.extend([("scores", u), ("shift", u)])
        prev = u - 1 if u else -1
        has_prev = u not in (0, 8) or (u == 0 and not first)
        if has_prev:
            finish(prev)
        if v % 2 == 0:
            out.append(("h_again", layer, b))
        out.append(("exp", u))
        if u == 0 and not first:
            out.append(("mask", 0, 3))
        if u == 1:
            if not first:
                out.extend([("ln_row", -1, 3), ("apply", -1, 3)])
            if not last:
                out.append(("load_adj",))
        if v in (3, 5, 7):
            out.extend([("ln_row", layer, (v - 3) // 2), ("apply", layer, (v - 3) // 2)])
        if not last and u in (4, 6):
            out.extend([("ln_x", (u - 4) // 2), ("relu_x", (u - 4) // 2)])
        if layer == 0:
            for h in halves[u:u + 1]:
                out.append(h)
                if h[2] == 1:
                    out.append(("evac", h[1]))
        elif not last:
            for h in halves[24 + 3 * v:27 + 3 * v]:
                out.append(h)
                if h[2] == 1:
                    out.append(("evac", h[1]))
        if has_prev:
            values(prev)
        if u == 0:
            out.append(("load_h", 0, 1))
            if not last:
                out.extend([("load_x", 0), ("load_x", 1)])
        if v >= 2 and v % 2 == 0:
            nb = v // 2 + 1
            if nb < GB:
                out.append(("load_h", layer, nb))
            elif layer == 0:
                out.append(("load_h", 1, 0))
            elif not last:
                out.append(("load_h", 2, 0))
        if not last and layer == 1 and v in (2, 4, 6):
            out.append(("mask", 1, v // 2 - 1))
        if not last and u == 15:
            out.append(("keep_stats",))
        if layer == 0 and v in (4, 6):
            out.extend([("t_edge", v // 2 - 2), ("t_evac", "edge", v // 2 - 2)])
        if u == 7:
            finish(7)
            tile("ev", 0, (0,))
            values(7)
            out.append(("load_h", 1, 1))
            out.append(("ln_row", 0, 3))
            tile("ev", 0, (1,))
            out.extend([("t_edge", 2), ("t_evac", "edge", 2)])
            tile("ev", 1)
            out.append(("apply", 0, 3))
            if not last:
                out.extend([("t_h", 0), ("t_evac", "h", 0), ("load_x", 2)])
            tile("ev", 2, (0,))
            out.extend([("t_edge", 3), ("t_evac", "edge", 3)])
            tile("ev", 2, (1,))
            tile("ek", 0)
            if not last:
                out.extend([("t_h", 1), ("t_evac", "h", 1), ("load_x", 3), ("ln_x", 2), ("relu_x", 2)])
            tile("ek", 1)
            tile("ek", 2)
            if not last:
                out.extend([("t_h", 2), ("t_evac", "h", 2), ("ln_x", 3), ("relu_x", 3)])
            tile("ek", 3)
            if not last:
                out.extend([("t_h", 3), ("t_evac", "h", 3)])
            tile("ev", 3)
    return out


def transpose_index(kind, b, last):
    if last:
        return b
    return {"edge": (0, 1, 2, 4), "h": (3, 5, 6, 7)}[kind][b]


def wait(eng, sem, value):
    if isinstance(value, int) and value <= 0:
        return
    eng.wait_ge(sem, value)


def wait_alone(eng, sem, value):
    if isinstance(value, int) and value <= 0:
        return
    eng.wait_ge(sem, value)
    eng.nop(nofuse=True)


def attention_pass(nc, x, adj, w, cols, rows_in, n2):
    ngroups = x.shape[0] // GB
    W_ORDER = ["q", "k", "v", "q2", "ek", "ev"]
    COL = {"q": 0, "k": 1, "q2": 2, "ek": 3, "g1": 4, "b1": 5}
    x_v = x.rearrange("(g b) p d -> g b p d", b=GB)
    n2_v = n2.rearrange("(g b) p d -> g b p d", b=GB)
    adj_v = adj.rearrange("(g b) i j -> g i b j", b=GB)

    def graph(view, g, b):
        if isinstance(g, int):
            return view[g, b]
        return view[bass.ds(g, 1), b].rearrange("o p d -> (o p) d")

    ctx = ExitStack()
    with ctx:
        def sb(name, shape, dt=F32):
            return ctx.enter_context(nc.sbuf_tensor(name, shape, dt))

        def sem(name):
            return ctx.enter_context(nc.semaphore(name))

        w_hi = {k: sb(f"w_{k}_hi", [P, KT, D], F32R) for k in W_ORDER}
        w_lo = {k: sb(f"w_{k}_lo", [P, KT, D], F32R) for k in W_ORDER}
        hT_hi, hT_lo = sb("hT_hi", [P, KT, R], F32R), sb("hT_lo", [P, KT, R], F32R)
        eT_hi, eT_lo = sb("eT_hi", [P, KT, R], F32R), sb("eT_lo", [P, KT, R], F32R)
        proj = {k: sb(f"proj_{k}", [P, KT, R]) for k in ("q", "k", "q2", "ek")}
        val = {k: sb(f"val_{k}", [P, GB, H, HV]) for k in ("v", "ev")}
        h_row = [sb(f"h_row{i}", [P, D]) for i in range(2)]
        x_row = [sb(f"x_row{i}", [P, D]) for i in range(2)]
        row = [sb(f"row{i}", [P, D]) for i in range(2)]
        prob = [sb(f"prob{i}", [P, HU * P]) for i in range(2)]
        probT = [sb(f"probT{i}", [P, HU * P]) for i in range(2)]
        bias_row = {"v": sb("bias_v", [P, D]), "ev": sb("bias_ev", [P, D])}
        col = sb("col", [P, 6, KT])
        adj_in = sb("adj_in", [P, GB, P])
        mask = sb("mask", [P, GB, P], BF16)
        ident = sb("ident", [P, P])
        ident_b = sb("ident_b", [P, P], BF16)
        neg_half = sb("neg_half", [P, 1])
        peak = sb("peak", [P, 2, HU])
        recip = sb("recip", [P, 2, HU])
        st_row, st_x = sb("st_row", [P, 6]), sb("st_x", [P, 6])
        mv_row, mv_x = sb("mv_row", [P, 2, 2]), sb("mv_x", [P, 2, 2])
        var_row, var_x = sb("var_row", [P, 1]), sb("var_x", [P, 1])
        ln_row = sb("ln_row", [P, 2, 2])
        ln_next, ln_cur = sb("ln_next", [P, GB, 2]), sb("ln_cur", [P, GB, 2])

        bank = [ctx.enter_context(nc.psum_tensor(f"bank{i}", [P, 512], F32)) for i in range(8)]
        ps_scores, ps_tile, ps_av = bank[0:2], bank[2:4], bank[4:6]
        ps_probT, ps_turn = bank[6], bank[7]

        s_const = sem("s_const")
        s_ident0, s_ident = sem("s_ident0"), sem("s_ident")
        s_ones = sem("s_ones")
        s_stage = [sem(f"s_stage{i}") for i in range(2)]
        s_matvec = sem("s_matvec")
        s_bias = sem("s_bias")
        s_fold = sem("s_fold")
        s_whi, s_wlo = sem("s_whi"), sem("s_wlo")
        s_adj = sem("s_adj")
        s_mask = sem("s_mask")
        s_xin = [sem(f"s_xin{i}") for i in range(2)]
        s_hin = [sem(f"s_hin{i}") for i in range(2)]
        s_hagain = sem("s_hagain")
        s_scores, s_peak, s_shift, s_exp = sem("s_scores"), sem("s_peak"), sem("s_shift"), sem("s_exp")
        s_pt, s_pt_evac = sem("s_pt"), sem("s_pt_evac")
        s_av, s_recip, s_norm, s_add = sem("s_av"), sem("s_recip"), sem("s_norm"), sem("s_add")
        s_tile = sem("s_tile")
        s_evac = [sem(f"s_evac{i}") for i in range(2)]
        s_turn, s_turn_hi, s_turn_lo = sem("s_turn"), sem("s_turn_hi"), sem("s_turn_lo")
        s_bn_row, s_mv_row, s_var_row, s_rstd_row, s_ln_row = (sem(f"s_{n}_row") for n in ("bn", "mv", "var", "rstd", "ln"))
        s_bn_x, s_mv_x, s_var_x, s_rstd_x, s_ln_x = (sem(f"s_{n}_x") for n in ("bn", "mv", "var", "rstd", "ln"))
        s_apply, s_relu, s_keep = sem("s_apply"), sem("s_relu"), sem("s_keep")
        s_store = [sem(f"s_store{i}") for i in range(2)]

        def turn_no(g, kind, b, last):
            return GB + TRANSPOSES * g + transpose_index(kind, b, last)

        def wait_tile(eng, g, t):
            wait(eng, s_evac[t % 2], (PRO_TILES + TILES * g) // 2 + t // 2 + 1 if isinstance(g, int)
                 else g * (TILES // 2) + (PRO_TILES // 2 + t // 2 + 1))

        def parity_heads(ap, par):
            return ap.rearrange("p (j two d) -> p two j d", two=2, d=HD)[:, par]

        def run_groups(eng, body):
            body(0, True, False)
            with eng.Fori(1, ngroups - 1) as g:
                body(g, False, False)
            body(ngroups - 1, False, True)

        block = ctx.enter_context(nc.Block())

        @block.sync
        def _(sp):
            def load_x(g, b):
                sp.dma_start(x_row[b % 2][:, :], graph(x_v, g, b)).then_inc(s_xin[b % 2], 16)

            def load_h(g, b):
                sp.dma_start(h_row[b % 2][:, :], graph(x_v, g, b)).then_inc(s_hin[b % 2], 16)

            def load_adj(g):
                src = adj_v[g] if isinstance(g, int) else adj_v[bass.ds(g, 1)].rearrange("o i b j -> (o i) b j")
                sp.dma_start(adj_in[:, :, :], src).then_inc(s_adj, 16)

            def store_n2(g, b):
                sp.dma_start(graph(n2_v, g, b), row[b % 2][:, :]).then_inc(s_store[b % 2], 16)

            load_x(0, 0)
            load_x(0, 1)
            sp.dma_start(col[:, :, :], cols).then_inc(s_const, 16)
            for k, src in zip(("v", "ev"), rows_in):
                sp.dma_start(bias_row[k][:, :], src.partition_broadcast(P)).then_inc(s_const, 16)
            load_adj(0)
            stage = (proj["q2"], proj["ek"])
            for i, k in enumerate(W_ORDER):
                if i >= 2:
                    sp.wait_ge(s_wlo, i - 1)
                sp.dma_start(stage[i % 2][:, :, :], w[k].rearrange("(k p) n -> p k n", p=P)).then_inc(s_stage[i % 2], 16)
                if i < 2:
                    sp.wait_ge(s_turn, i + 1)
                    load_x(0, i + 2)
            load_h(0, 0)

            def body(g, first, last):
                for step in steps_of_group(first, last):
                    if step[0] == "load_x":
                        b = step[1]
                        if b < 2:
                            wait_alone(sp, s_turn, 4 if first else turn_no(g - 1, "h", b + 2, False) + 1)
                        else:
                            wait_alone(sp, s_turn, turn_no(g, "h", b - 2, False) + 1)
                        load_x(g + 1, b)
                    elif step[0] == "load_h":
                        layer, b = step[1:]
                        unit = 8 * layer + 2 * b - 3
                        wait_alone(sp, s_add, g * UNITS + unit + 1 if not (first and unit < 0) else 0)
                        load_h(g + 1 if layer == 2 else g, b)
                    elif step[0] == "load_adj":
                        wait_alone(sp, s_mask, g * GB + GB)
                        load_adj(g + 1)
                    elif step[0] == "apply" and step[1] != 0:
                        gg, b = (g, step[2]) if step[1] == 1 else (g - 1, 3)
                        wait_alone(sp, s_apply, gg * 8 + 4 + b + 1)
                        store_n2(gg, b)
            run_groups(sp, body)
            sp.wait_ge(s_apply, 8 * ngroups)
            store_n2(ngroups - 1, 3)
            for i in range(2):
                sp.wait_ge(s_store[i], 16 * 2 * ngroups)

        @block.gpsimd
        def _(pool):
            nc.gpsimd.memset(ident[:, :], 0.0).then_inc(s_ident0, 1)
            nc.gpsimd.memset(ident_b[:, :], 0.0).then_inc(s_ident0, 1)
            nc.gpsimd.memset(neg_half[:, :], -0.5).then_inc(s_ident0, 1)
            pool.wait_ge(s_ident0, 3)
            for m in (ident, ident_b):
                nc.gpsimd.affine_select(out=m[:, :], in_=m[:, :], compare_op=ALU.not_equal, fill=1.0,
                                        base=0, pattern=[[-1, P]], channel_multiplier=1).then_inc(s_ident, 1)

            def make_mask(g, b):
                wait_alone(pool, s_adj, g * 16 + 16)
                nc.gpsimd.tensor_scalar(mask[:, b, :], adj_in[:, b, :], 0.0, MASKED, ALU.is_le, ALU.mult).then_inc(s_mask, 1)

            def norm_factors(n, mv, var, rstd, shift, s_mv, s_var, s_rstd, s_ln):
                wait_alone(pool, s_mv, n + 1)
                nc.gpsimd.tensor_scalar(var[:, :], mv[:, 1:2], LN_EPS, None, ALU.add).then_inc(s_var, 1)
                pool.wait_ge(s_var, n + 1)
                nc.gpsimd.tensor_tensor(rstd, var[:, :], neg_half[:, :], ALU.pow).then_inc(s_rstd, 1)
                wait_alone(pool, s_rstd, n + 1)
                nc.gpsimd.tensor_scalar(shift, mv[:, 0:1], rstd, -1.0, ALU.mult, ALU.mult).then_inc(s_ln, 1)

            def ln_x(n, b):
                norm_factors(n, mv_x[:, b % 2, :], var_x, ln_next[:, b, 0:1], ln_next[:, b, 1:2],
                             s_mv_x, s_var_x, s_rstd_x, s_ln_x)

            def ln_rows(n, b):
                if not (isinstance(n, int) and n < 2):
                    wait_alone(pool, s_apply, n - 1)
                norm_factors(n, mv_row[:, b % 2, :], var_row, ln_row[:, b % 2, 0:1], ln_row[:, b % 2, 1:2],
                             s_mv_row, s_var_row, s_rstd_row, s_ln_row)

            for b in range(GB):
                make_mask(0, b)
                ln_x(b, b)

            def body(g, first, last):
                for step in steps_of_group(first, last):
                    if step[0] == "mask":
                        b = step[2]
                        gg = g + step[1]
                        wait_alone(pool, s_scores, (gg - 1) * UNITS + 8 + 2 * b + 2)
                        make_mask(gg, b)
                    elif step[0] == "ln_x":
                        b = step[1]
                        wait_alone(pool, s_keep, g + 1)
                        ln_x(g * GB + (GB + b), b)
                    elif step[0] == "ln_row":
                        ln_rows(g * 8 + 4 * step[1] + step[2], step[2])
                    elif step[0] == "add_h":
                        u = step[1]
                        b, par = (u % 8) // 2, u % 2
                        n = g * UNITS + u
                        pool.wait_ge(s_norm, n + 1)
                        pool.wait_ge(s_hagain, g * 8 + u // 2 + 1)
                        out = parity_heads(row[b % 2][:, :], par)
                        nc.gpsimd.tensor_tensor(out, out, parity_heads(h_row[b % 2][:, :], par), ALU.add).then_inc(s_add, 1)
            run_groups(pool, body)
            n = ngroups * UNITS - 1
            pool.wait_ge(s_norm, n + 1)
            out = parity_heads(row[1][:, :], 1)
            nc.gpsimd.tensor_tensor(out, out, parity_heads(h_row[1][:, :], 1), ALU.add).then_inc(s_add, 1)
            ln_rows(ngroups * 8 - 1, 3)

        @block.scalar
        def _(act):
            def relu_x(n, b):
                act.wait_ge(s_ln_x, n + 1)
                nc.scalar.activation(x_row[b % 2][:, :], x_row[b % 2][:, :], ACT.Relu, bias=ln_next[:, b, 1:2],
                                     scale=ln_next[:, b, 0:1]).then_inc(s_relu, 1)

            def turn_hi(no, kind, b):
                dst = hT_hi if kind == "h" else eT_hi
                wait(act, s_turn, no + 1)
                nc.scalar.activation(dst[:, :, b * P:(b + 1) * P], ps_turn[:, :].rearrange("p (k r) -> p k r", k=KT),
                                     ACT.Copy).then_inc(s_turn_hi, 1)

            def split_hi(i):
                if i < 4:
                    act.wait_ge(s_stage[i % 2], 16 * (i // 2 + 1))
                else:
                    act.wait_ge(s_fold, i - 3)
                nc.scalar.activation(w_hi[W_ORDER[i]][:, :, :], (proj["q2"], proj["ek"])[i % 2][:, :, :],
                                     ACT.Copy).then_inc(s_whi, 1)

            def evac(no, t):
                kind, m = TILE_KIND[t]
                if kind in ("v", "ev"):
                    return
                wait(act, s_tile, no + 1)
                nc.scalar.activation(proj[kind][:, m, :], ps_tile[t % 2][:, :], ACT.Identity,
                                     bias=col[:, COL[kind], m:m + 1]).then_inc(s_evac[t % 2], 1)

            def keep():
                nc.scalar.activation(ln_cur[:, :, :], ln_next[:, :, :], ACT.Copy).then_inc(s_keep, 1)

            def apply(n, b):
                act.wait_ge(s_ln_row, n + 1)
                nc.scalar.activation(row[b % 2][:, :], row[b % 2][:, :], ACT.Identity, bias=ln_row[:, b % 2, 1:2],
                                     scale=ln_row[:, b % 2, 0:1]).then_inc(s_apply, 1)

            act.wait_ge(s_const, 48)
            for b in range(GB):
                relu_x(b, b)
                turn_hi(b, "h", b)
                if b < 2:
                    split_hi(b)
            keep()
            split_hi(2)
            split_hi(3)
            for t in range(TILES - PRO_TILES, TILES):
                evac(t - PRO_TILES, t)
            split_hi(4)
            split_hi(5)

            def pt_evac(n, u):
                act.wait_ge(s_pt, n + 1)
                nc.scalar.activation(probT[u % 2][:, :], ps_probT[:, :], ACT.Copy).then_inc(s_pt_evac, 1)

            def body(g, first, last):
                for step in steps_of_group(first, last):
                    if step[0] == "pt_evac":
                        pt_evac(g * UNITS + step[1], step[1] % UNITS)
                    elif step[0] == "h_again":
                        layer, b = step[1:]
                        act.wait_ge(s_hin[b % 2], g * 64 + 16 * (2 * layer + b // 2 + 1))
                        act.wait_ge(s_keep, g + 1)
                        nc.scalar.activation(h_row[b % 2][:, :], h_row[b % 2][:, :], ACT.Relu, bias=ln_cur[:, b, 1:2],
                                             scale=ln_cur[:, b, 0:1]).then_inc(s_hagain, 1)
                    elif step[0] == "exp":
                        u = step[1]
                        act.wait_ge(s_shift, g * UNITS + u + 1)
                        nc.scalar.activation(prob[u % 2][:, :], prob[u % 2][:, :], ACT.Exp, scale=SCALE).then_inc(s_exp, 1)
                    elif step[0] == "evac":
                        evac(g * TILES + (PRO_TILES + step[1]), step[1])
                    elif step[0] == "apply":
                        apply(g * 8 + 4 * step[1] + step[2], step[2])
                    elif step[0] == "relu_x":
                        relu_x(g * GB + (GB + step[1]), step[1])
                    elif step[0] == "t_evac":
                        turn_hi(turn_no(g, step[1], step[2], last), step[1], step[2])
                    elif step[0] == "keep_stats":
                        keep()
            run_groups(act, body)
            pt_evac(ngroups * UNITS - 1, UNITS - 1)
            apply(ngroups * 8 - 1, 3)

        @block.vector
        def _(dve):
            for k in ("v", "ev"):
                last_ones = nc.vector.memset(val[k][:, :, :, HD:HV], 1.0).then_inc(s_ones, 1)

            def stats(n, src, st, mv, s_bn, s_mv):
                nc.vector.bn_stats(st[:, :], src).then_inc(s_bn, 1)
                wait_alone(dve, s_bn, n + 1)
                nc.vector.bn_aggr(mv, st[:, :]).then_inc(s_mv, 1)

            def ln_x(g, n, b):
                dve.wait_ge(s_xin[b % 2], g * 32 + 16 * (b // 2 + 1))
                if not (isinstance(n, int) and n < 2):
                    dve.wait_ge(s_ln_x, n - 1)
                stats(n, x_row[b % 2][:, :], st_x, mv_x[:, b % 2, :], s_bn_x, s_mv_x)

            def ln_rows(n, b, unit_no):
                dve.wait_ge(s_add, unit_no + 1)
                stats(n, row[b % 2][:, :], st_row, mv_row[:, b % 2, :], s_bn_row, s_mv_row)

            def turn_lo(no, kind, b):
                hi, lo = (hT_hi, hT_lo) if kind == "h" else (eT_hi, eT_lo)
                dve.wait_ge(s_turn_hi, no + 1)
                nc.vector.tensor_tensor(lo[:, :, b * P:(b + 1) * P], ps_turn[:, :].rearrange("p (k r) -> p k r", k=KT),
                                        hi[:, :, b * P:(b + 1) * P].bitcast(F32), ALU.subtract).then_inc(s_turn_lo, 1)

            def split_lo(i):
                k = W_ORDER[i]
                stage = (proj["q2"], proj["ek"])[i % 2]
                if i >= 4:
                    dve.wait_ge(s_stage[i % 2], 16 * (i // 2 + 1))
                    dve.wait_ge(s_matvec, i - 3)
                    if k == "ek":
                        nc.vector.tensor_tensor(col[:, COL["ek"], :], ps_av[0][:, 0:KT], col[:, COL["ek"], :],
                                                ALU.add).then_inc(s_bias, 1)
                    else:
                        nc.vector.tensor_tensor(bias_row["ev"][:, :], ps_av[1][:, :], bias_row["ev"][:, :],
                                                ALU.add).then_inc(s_bias, 1)
                    for t in range(KT):
                        folded = nc.vector.tensor_scalar(stage[:, t, :], stage[:, t, :], col[:, COL["g1"], t:t + 1],
                                                         None, ALU.mult)
                    folded.then_inc(s_fold, 1)
                dve.wait_ge(s_whi, i + 1)
                nc.vector.tensor_tensor(w_lo[k][:, :, :], stage[:, :, :], w_hi[k][:, :, :].bitcast(F32),
                                        ALU.subtract).then_inc(s_wlo, 1)

            def evac(no, t):
                kind, b = TILE_KIND[t]
                if kind not in ("v", "ev"):
                    return
                wait(dve, s_tile, no + 1)
                nc.vector.tensor_tensor(val[kind][:, b, :, 0:HD], ps_tile[t % 2][:, :].rearrange("p (h d) -> p h d", h=H),
                                        bias_row[kind][:, :].rearrange("p (h d) -> p h d", h=H),
                                        ALU.add).then_inc(s_evac[t % 2], 1)

            dve.wait_ge(s_const, 48)
            for b in range(GB):
                ln_x(0, b, b)
                turn_lo(b, "h", b)
                if b < 2:
                    split_lo(b)
            split_lo(2)
            split_lo(3)
            for t in range(TILES - PRO_TILES, TILES):
                evac(t - PRO_TILES, t)
            split_lo(4)
            split_lo(5)
            dve.wait_ge(s_bias, 2)

            def normalise(g, n, u):
                layer, b, par = (u % UNITS) // 8, (u % 8) // 2, u % 2
                dve.wait_ge(s_av, n + 1)
                src = ps_av[par][:, 0:HU * HV].rearrange("p (j d) -> p j d", d=HV)
                nc.vector.reciprocal(recip[:, par, :], src[:, :, HD]).then_inc(s_recip, 1)
                if par == 0:
                    if layer == 0 and b >= 2:
                        dve.wait_ge(s_turn, turn_no(g, "edge", b - 2, u_last[0]) + 1)
                    elif layer == 0:
                        wait(dve, s_store[b % 2], g * 32)
                    elif b < 2:
                        dve.wait_ge(s_turn, turn_no(g, "edge", b + 2, u_last[0]) + 1)
                    else:
                        dve.wait_ge(s_store[b % 2], g * 32 + 16)
                dve.wait_ge(s_recip, n + 1)
                nc.vector.tensor_tensor(parity_heads(row[b % 2][:, :], par), src[:, :, 0:HD],
                                        recip[:, par, :].unsqueeze(2).broadcast_to([P, HU, HD]), ALU.mult).then_inc(s_norm, 1)

            u_last = [False]

            def body(g, first, last):
                u_last[0] = last
                for step in steps_of_group(first, last):
                    if step[0] == "shift":
                        u = step[1]
                        n = g * UNITS + u
                        src = ps_scores[u % 2][:, :].rearrange("p (j k) -> p j k", j=HU)
                        dve.wait_ge(s_scores, n + 1)
                        nc.vector.tensor_reduce(peak[:, u % 2, :], src, AX.X, ALU.max).then_inc(s_peak, 1)
                        if not (first and u < 2):
                            dve.wait_ge(s_pt, n - 1)
                        dve.wait_ge(s_peak, n + 1)
                        nc.vector.tensor_tensor(prob[u % 2][:, :].rearrange("p (j k) -> p j k", j=HU), src,
                                                peak[:, u % 2, :].unsqueeze(2).broadcast_to([P, HU, P]),
                                                ALU.subtract).then_inc(s_shift, 1)
                    elif step[0] == "norm":
                        normalise(g, g * UNITS + step[1], step[1])
                    elif step[0] == "evac":
                        evac(g * TILES + (PRO_TILES + step[1]), step[1])
                    elif step[0] == "ln_row":
                        layer, b = step[1:]
                        ln_rows(g * 8 + 4 * layer + b, b, g * UNITS + 8 * layer + 2 * b + 1)
                    elif step[0] == "ln_x":
                        ln_x(g + 1, g * GB + (GB + step[1]), step[1])
                    elif step[0] == "t_evac":
                        turn_lo(turn_no(g, step[1], step[2], last), step[1], step[2])
            run_groups(dve, body)
            normalise(ngroups, ngroups * UNITS - 1, -1)
            ln_rows(ngroups * 8 - 1, 3, ngroups * UNITS - 1)

        @block.tensor
        def _(pe):
            def turn(no, src, ready, count):
                wait(pe, ready, count)
                wait(pe, s_turn_lo, no)
                for k in range(KT):
                    last = nc.tensor.transpose(ps_turn[:, k * P:(k + 1) * P], src[:, k * P:(k + 1) * P], ident[:, :])
                last.then_inc(s_turn, 1)

            def half_tile(g, t, part):
                kind, m = TILE_KIND[t]
                hi, lo = (eT_hi, eT_lo) if kind in ("ek", "ev") else (hT_hi, hT_lo)
                if part == 0:
                    wait(pe, s_evac[t % 2], g * (TILES // 2) + (PRO_TILES // 2 + t // 2))
                for k in range(2 * part, 2 * part + 2):
                    for a, c in (("hi", "hi"), ("hi", "lo"), ("lo", "hi")):
                        if kind in ("v", "ev"):
                            lhsT = (hi if a == "hi" else lo)[:, k, m * P:(m + 1) * P]
                            rhs = (w_hi if c == "hi" else w_lo)[kind][:, k, :]
                        else:
                            lhsT = (w_hi if a == "hi" else w_lo)[kind][:, k, m * P:(m + 1) * P]
                            rhs = (hi if c == "hi" else lo)[:, k, :]
                        last = nc.tensor.matmul(ps_tile[t % 2][:, :], lhsT, rhs, start=(k == 0 and a + c == "hihi"),
                                                stop=(k == KT - 1 and a == "lo"))
                if part == 1:
                    last.then_inc(s_tile, 1)

            pe.wait_ge(s_ident, 2)
            for b in range(GB):
                turn(b, x_row[b % 2], s_relu, b + 1)
            pe.wait_ge(s_turn_lo, GB)
            for t in range(TILES - PRO_TILES, TILES):
                pe.wait_ge(s_wlo, {"q": 1, "k": 2, "v": 3}[TILE_KIND[t][0]])
                half_tile(-1, t, 0)
                half_tile(-1, t, 1)
            pe.wait_ge(s_stage[0], 48)
            for m in range(KT):
                for k in range(KT):
                    last = nc.tensor.matmul(ps_av[0][:, m:m + 1], proj["q2"][:, k, m * P:(m + 1) * P],
                                            col[:, COL["b1"], k:k + 1], start=(k == 0), stop=(k == KT - 1))
            last.then_inc(s_matvec, 1)
            pe.wait_ge(s_stage[1], 48)
            for k in range(KT):
                last = nc.tensor.matmul(ps_av[1][:, :], col[:, COL["b1"], k:k + 1].broadcast_to([P, P]),
                                        proj["ek"][:, k, :], start=(k == 0), stop=(k == KT - 1))
            last.then_inc(s_matvec, 1)
            pe.wait_ge(s_wlo, 6)
            pe.wait_ge(s_bias, 2)
            pe.wait_ge(s_ones, 2)

            def transpose_probs(n, u):
                pe.wait_ge(s_exp, n + 1)
                wait(pe, s_pt_evac, n)
                for j in range(HU):
                    last = nc.tensor.transpose(ps_probT[:, j * P:(j + 1) * P], prob[u % 2][:, j * P:(j + 1) * P], ident[:, :])
                last.then_inc(s_pt, 1)

            def attend(g, n, u):
                layer, b, par = (u % UNITS) // 8, (u % 8) // 2, u % 2
                pe.wait_ge(s_pt_evac, n + 1)
                wait(pe, s_norm, n - 1)
                if layer == 0 and u % UNITS < 2:
                    wait_tile(pe, g - 1, TILE_OF[("v", 2)])
                    wait_tile(pe, g - 1, TILE_OF[("v", 3)])
                elif layer == 1 and par == 0:
                    wait_tile(pe, g, TILE_OF[("ev", b)])
                for j in range(HU):
                    last = nc.tensor.matmul(ps_av[par][:, j * HV:(j + 1) * HV], probT[u % 2][:, j * P:(j + 1) * P],
                                            val[("v", "ev")[layer]][:, b, 2 * j + par, :], start=True, stop=True)
                last.then_inc(s_av, 1)

            def body(g, first, last):
                for step in steps_of_group(first, last):
                    if step[0] == "scores":
                        u = step[1]
                        layer, b, par = u // 8, (u % 8) // 2, u % 2
                        n = g * UNITS + u
                        if not (first and u < 2):
                            pe.wait_ge(s_shift, n - 1)
                        if layer == 0 and par == 0:
                            pe.wait_ge(s_mask, g * GB + (b + 1))
                        if layer == 0 and u == 0:
                            wait_tile(pe, g - 1, TILE_OF[("q", 3)])
                            wait_tile(pe, g - 1, TILE_OF[("k", 3)])
                        if layer == 1 and u == 8:
                            wait_tile(pe, g, TILE_OF[("ek", 3)])
                            wait_tile(pe, g, TILE_OF[("ek", 2)])
                        every = (lambda ap: ap.unsqueeze(1).broadcast_to([P, HU, P]))
                        out = ps_scores[u % 2]
                        if layer == 0:
                            nc.tensor.matmul(out[:, :], mask[:, b, :], every(ident_b[:, :]), start=True, stop=False)
                        else:
                            nc.tensor.matmul(out[:, :], ident_b[:, :], every(mask[:, b, :]), start=True, stop=False)
                        q, k = (proj["q"], proj["k"]) if layer == 0 else (proj["q2"], proj["ek"])
                        half = slice(HD * par, HD * (par + 1))
                        for j in range(HU):
                            mm = nc.tensor.matmul(out[:, j * P:(j + 1) * P], q[half, j, b * P:(b + 1) * P],
                                                  k[half, j, b * P:(b + 1) * P], start=False, stop=(j == HU - 1))
                        mm.then_inc(s_scores, 1)
                    elif step[0] == "pt":
                        transpose_probs(g * UNITS + step[1], step[1] % UNITS)
                    elif step[0] == "av":
                        attend(g, g * UNITS + step[1], step[1] % UNITS)
                    elif step[0] == "half":
                        t, part = step[1:]
                        if part == 0 and TILE_KIND[t][0] in ("ev", "ek", "q"):
                            kind, m = TILE_KIND[t]
                            turned = ("edge", m) if kind == "ev" else ("edge", 3) if kind == "ek" else ("h", 3)
                            pe.wait_ge(s_turn_lo, turn_no(g, *turned, last) + 1)
                        half_tile(g, t, part)
                    elif step[0] == "t_edge":
                        b = step[1]
                        turn(turn_no(g, "edge", b, last), row[b % 2], s_apply, g * 8 + (b + 1))
                    elif step[0] == "t_h":
                        b = step[1]
                        turn(turn_no(g, "h", b, last), x_row[b % 2], s_relu, g * GB + (GB + b + 1))
            run_groups(pe, body)
            transpose_probs(ngroups * UNITS - 1, UNITS - 1)
            attend(ngroups - 1, ngroups * UNITS - 1, UNITS - 1)


def ffn_steps(g_first, g_last, prep):
    out = []
    for t in range(FT):
        out.extend([("up", t), ("gelu", t)])
        if prep and t + 2 < FT:
            out.extend([("prep", t + 2)])
        if t or not g_first:
            out.append(("down", t - 1))
        out.append(("split", t))
        if t == 0 and not g_first:
            out.extend([("add_res", mt) for mt in range(GB)])
        if t in (2, 3) and not g_first:
            out.append(("load_x", -1, t))
        if 1 <= t <= GB and not g_first:
            out.extend([("finish", t - 1)])
        if 5 <= t < 5 + GB and not g_last and not g_first:
            out.append(("load_n2", t - 5))
        if t in (9, 10):
            out.append(("load_x", 0, t - 9))
        if t == FT - 2 and g_first and not g_last:
            out.extend([("load_n2", b) for b in range(GB)])
        if not g_last:
            at = (8, 10, 12, 14) if not g_first else (15, 15, 15, 15)
            out.extend([("turn", b) for b in range(GB) if at[b] == t])
    return out


def ffn_pass(nc, n2, x, w1, w2, cols, rows_in, out):
    cols_n, cols_b = cols
    ngroups = x.shape[0] // GB
    x_v = x.rearrange("(g b) p d -> g b p d", b=GB)
    n2_v = n2.rearrange("(g b) p d -> g b p d", b=GB)
    out_v = out.rearrange("(g b) p d -> g b p d", b=GB)
    w1_v = w1.rearrange("(k p) (t n) -> t p k n", p=P, n=P)
    w2_v = w2.rearrange("(t p) n -> t p n", p=P)

    def graph(view, g, b):
        if isinstance(g, int):
            return view[g, b]
        return view[bass.ds(g, 1), b].rearrange("o p d -> (o p) d")

    ctx = ExitStack()
    with ctx:
        def sb(name, shape, dt=F32):
            return ctx.enter_context(nc.sbuf_tensor(name, shape, dt))

        def sem(name):
            return ctx.enter_context(nc.semaphore(name))

        w1_hi, w1_lo = sb("w1_hi", [P, KT, DF], F32R), sb("w1_lo", [P, KT, DF], F32R)
        w2_hi, w2_lo = sb("w2_hi", [P, FT, D], F32R), sb("w2_lo", [P, FT, D], F32R)
        nT_hi = [sb(f"nT_hi{i}", [P, KT, R], F32R) for i in range(2)]
        nT_lo = [sb(f"nT_lo{i}", [P, KT, R], F32R) for i in range(2)]
        n_row = [sb(f"n_row{i}", [P, GB, D]) for i in range(2)]
        x_res = [sb(f"x_res{i}", [P, D]) for i in range(2)]
        act_f = [sb(f"act_f{i}", [P, R]) for i in range(2)]
        act_hi = [sb(f"act_hi{i}", [P, R], F32R) for i in range(2)]
        act_lo = [sb(f"act_lo{i}", [P, R], F32R) for i in range(2)]
        gain2, shift2 = sb("gain2", [P, D]), sb("shift2", [P, D])
        gain3, shift3 = sb("gain3", [P, D]), sb("shift3", [P, D])
        bias_down = act_f[1]
        col = sb("fcol", [P, 2, KT])
        bias_up = sb("bias_up", [P, FT])
        ident = sb("fident", [P, P])
        neg_half = sb("fneg_half", [P, 1])
        st = sb("fst", [P, 2, 6])
        mv = sb("fmv", [P, 2, 2])
        var = sb("fvar", [P, 1])
        ln = sb("fln", [P, 2, 2])

        bank = [ctx.enter_context(nc.psum_tensor(f"fbank{i}", [P, 512], F32)) for i in range(8)]
        ps_up, ps_down, ps_turn, ps_vec = bank[0:2], bank[2:6], bank[6], bank[7]

        s_const = sem("f_const")
        s_ident0, s_ident = sem("f_ident0"), sem("f_ident")
        s_shift2 = sem("f_shift2")
        s_w1in = [sem(f"f_w1in{i}") for i in range(2)]
        s_w2in = [sem(f"f_w2in{i}") for i in range(2)]
        s_matvec, s_bias, s_fold = sem("f_matvec"), sem("f_bias"), sem("f_fold")
        s_whi, s_wlo = sem("f_whi"), sem("f_wlo")
        s_n2in = [sem(f"f_n2in{b}") for b in range(GB)]
        s_xin = [sem(f"f_xin{i}") for i in range(2)]
        s_turn, s_turn_hi, s_turn_lo = sem("f_turn"), sem("f_turn_hi"), sem("f_turn_lo")
        s_gain, s_res = sem("f_gain"), sem("f_res")
        s_up, s_gelu, s_act_hi, s_act = sem("f_up"), sem("f_gelu"), sem("f_act_hi"), sem("f_act")
        s_down = sem("f_down")
        s_sum = sem("f_sum")
        s_bn, s_mv, s_var, s_rstd, s_ln = (sem(f"f_{n}") for n in ("bn", "mv", "var", "rstd", "ln"))
        s_apply, s_gain3, s_xb, s_out = sem("f_apply"), sem("f_gain3"), sem("f_xb"), sem("f_out")
        s_store = [sem(f"f_store{b}") for b in range(GB)]

        stage1 = [n_row[1][:, 2 * i, :].rearrange("p (k n) -> p k n", k=KT) for i in range(2)]
        stage2 = [n_row[1][:, 2 * i + 1, :] for i in range(2)]

        def run_pairs(eng, body):
            body(0, 0, True, False)
            body(1, 1, False, False)
            with eng.Fori(1, ngroups // 2 - 1) as pair:
                body(pair * 2, 0, False, False)
                body(pair * 2 + 1, 1, False, False)
            body(ngroups - 2, 0, False, False)
            body(ngroups - 1, 1, False, True)

        block = ctx.enter_context(nc.Block())

        @block.sync
        def _(sp):
            def load_n2(g, par, b):
                sp.dma_start(n_row[par][:, b, :], graph(n2_v, g, b)).then_inc(s_n2in[b], 16)

            def load_x(g, b):
                sp.dma_start(x_res[b % 2][:, :], graph(x_v, g, b)).then_inc(s_xin[b % 2], 16)

            def load_weights(t):
                if t >= 2:
                    sp.wait_ge(s_wlo, 2 * (t - 1))
                sp.dma_start(stage1[t % 2], w1_v[t]).then_inc(s_w1in[t % 2], 16)
                sp.dma_start(stage2[t % 2], w2_v[t]).then_inc(s_w2in[t % 2], 16)

            def store(g, par, b):
                wait_alone(sp, s_out, g * GB + (b + 1))
                sp.dma_start(graph(out_v, g, b), n_row[par][:, b, :]).then_inc(s_store[b], 16)

            for b in range(GB):
                load_n2(0, 0, b)
                if b == 0:
                    sp.dma_start(col[:, :, :], cols_n).then_inc(s_const, 16)
                    sp.dma_start(bias_up[:, :], cols_b).then_inc(s_const, 16)
                    load_weights(0)
                    load_weights(1)
            for dst, src in zip((gain2[:, :], shift2[:, :], bias_down[:, :], gain3[:, :], shift3[:, :]), rows_in):
                sp.dma_start(dst, src.partition_broadcast(P)).then_inc(s_const, 16)

            def body(g, par, first, last):
                for step in ffn_steps(first, last, first):
                    if step[0] == "prep":
                        load_weights(step[1])
                    elif step[0] == "load_n2":
                        b = step[1]
                        if first:
                            sp.wait_ge(s_wlo, 2 * FT)
                        else:
                            wait_alone(sp, s_store[b], g * 16)
                        load_n2(g + 1, 1 - par, b)
                    elif step[0] == "load_x":
                        gg, b = g + step[1], step[2]
                        wait_alone(sp, s_out, gg * GB + (b - 1))
                        load_x(gg, b)
                    elif step[0] == "finish":
                        store(g - 1, 1 - par, step[1])
            run_pairs(sp, body)
            for b in range(GB):
                store(ngroups - 1, 1, b)
                if b < 2:
                    load_x(ngroups - 1, b + 2)
            for b in range(GB):
                sp.wait_ge(s_store[b], 16 * ngroups)

        @block.gpsimd
        def _(pool):
            nc.gpsimd.memset(ident[:, :], 0.0).then_inc(s_ident0, 1)
            nc.gpsimd.memset(neg_half[:, :], -0.5).then_inc(s_ident0, 1)
            pool.wait_ge(s_ident0, 2)
            nc.gpsimd.affine_select(out=ident[:, :], in_=ident[:, :], compare_op=ALU.not_equal, fill=1.0,
                                    base=0, pattern=[[-1, P]], channel_multiplier=1).then_inc(s_ident, 1)
            pool.wait_ge(s_const, 16 * 7)
            nc.gpsimd.tensor_tensor(shift2[:, :], shift2[:, :], bias_down[:, :], ALU.add).then_inc(s_shift2, 1)
            pool.wait_ge(s_shift2, 1)

            def residual(n, par, b):
                pool.wait_ge(s_turn, n + 1)
                nc.gpsimd.tensor_tensor(n_row[par][:, b, :], n_row[par][:, b, :], gain2[:, :], ALU.mult).then_inc(s_gain, 1)
                pool.wait_ge(s_gain, n + 1)
                nc.gpsimd.tensor_tensor(n_row[par][:, b, :], n_row[par][:, b, :], shift2[:, :], ALU.add).then_inc(s_res, 1)

            def finish(g, par, b):
                n = g * GB + b
                wait_alone(pool, s_mv, n + 1)
                nc.gpsimd.tensor_scalar(var[:, :], mv[:, b % 2, 1:2], LN_EPS, None, ALU.add).then_inc(s_var, 1)
                pool.wait_ge(s_var, n + 1)
                if not (isinstance(g, int) and n < 2):
                    pool.wait_ge(s_apply, n - 1)
                nc.gpsimd.tensor_tensor(ln[:, b % 2, 0:1], var[:, :], neg_half[:, :], ALU.pow).then_inc(s_rstd, 1)
                wait_alone(pool, s_rstd, n + 1)
                nc.gpsimd.tensor_scalar(ln[:, b % 2, 1:2], mv[:, b % 2, 0:1], ln[:, b % 2, 0:1], -1.0,
                                        ALU.mult, ALU.mult).then_inc(s_ln, 1)
                pool.wait_ge(s_xin[b % 2], g * 32 + 16 * (b // 2 + 1))
                nc.gpsimd.tensor_tensor(x_res[b % 2][:, :], x_res[b % 2][:, :], shift3[:, :], ALU.add).then_inc(s_xb, 1)
                pool.wait_ge(s_apply, n + 1)
                nc.gpsimd.tensor_tensor(n_row[par][:, b, :], n_row[par][:, b, :], gain3[:, :], ALU.mult).then_inc(s_gain3, 1)
                pool.wait_ge(s_gain3, n + 1)
                pool.wait_ge(s_xb, n + 1)
                nc.gpsimd.tensor_tensor(n_row[par][:, b, :], n_row[par][:, b, :], x_res[b % 2][:, :], ALU.add).then_inc(s_out, 1)

            for b in range(GB):
                residual(b, 0, b)

            def body(g, par, first, last):
                for step in ffn_steps(first, last, first):
                    if step[0] == "turn":
                        residual(g * GB + (GB + step[1]), 1 - par, step[1])
                    elif step[0] == "finish":
                        finish(g - 1, 1 - par, step[1])
            run_pairs(pool, body)
            for b in range(GB):
                finish(ngroups - 1, 1, b)

        @block.scalar
        def _(act):
            def turn_hi(n, par, b):
                act.wait_ge(s_turn, n + 1)
                nc.scalar.activation(nT_hi[par][:, :, b * P:(b + 1) * P], ps_turn[:, :].rearrange("p (k r) -> p k r", k=KT),
                                     ACT.Copy).then_inc(s_turn_hi, 1)

            def prep_hi(t):
                act.wait_ge(s_fold, t + 1)
                nc.scalar.activation(w1_hi[:, :, t * P:(t + 1) * P], stage1[t % 2], ACT.Copy).then_inc(s_whi, 1)
                act.wait_ge(s_w2in[t % 2], 16 * (t // 2 + 1))
                nc.scalar.activation(w2_hi[:, t, :], stage2[t % 2], ACT.Copy).then_inc(s_whi, 1)

            def apply(n, par, b):
                act.wait_ge(s_ln, n + 1)
                nc.scalar.activation(n_row[par][:, b, :], n_row[par][:, b, :], ACT.Identity, bias=ln[:, b % 2, 1:2],
                                     scale=ln[:, b % 2, 0:1]).then_inc(s_apply, 1)

            act.wait_ge(s_const, 16 * 7)
            for b in range(GB):
                turn_hi(b, 0, b)
                if b < 2:
                    prep_hi(b)

            def body(g, par, first, last):
                for step in ffn_steps(first, last, first):
                    if step[0] == "gelu":
                        t = step[1]
                        n = g * FT + t
                        act.wait_ge(s_up, n + 1)
                        if first and t < 2:
                            act.wait_ge(s_shift2, 1)
                        else:
                            act.wait_ge(s_act, n - 1)
                        if first:
                            act.wait_ge(s_bias, t + 1)
                        nc.scalar.activation(act_f[t % 2][:, :], ps_up[t % 2][:, :], ACT.Gelu,
                                             bias=bias_up[:, t:t + 1]).then_inc(s_gelu, 1)
                    elif step[0] == "prep":
                        prep_hi(step[1])
                    elif step[0] == "turn":
                        turn_hi(g * GB + (GB + step[1]), 1 - par, step[1])
                    elif step[0] == "finish":
                        apply(g * GB + (step[1] - GB), 1 - par, step[1])
            run_pairs(act, body)
            for b in range(GB):
                apply((ngroups - 1) * GB + b, 1, b)

        @block.vector
        def _(dve):
            def turn_lo(n, par, b):
                dve.wait_ge(s_turn_hi, n + 1)
                nc.vector.tensor_tensor(nT_lo[par][:, :, b * P:(b + 1) * P], ps_turn[:, :].rearrange("p (k r) -> p k r", k=KT),
                                        nT_hi[par][:, :, b * P:(b + 1) * P].bitcast(F32), ALU.subtract).then_inc(s_turn_lo, 1)

            def prep(t):
                dve.wait_ge(s_matvec, t + 1)
                nc.vector.tensor_tensor(bias_up[:, t:t + 1], ps_vec[:, t:t + 1], bias_up[:, t:t + 1], ALU.add).then_inc(s_bias, 1)
                nc.vector.tensor_tensor(stage1[t % 2], stage1[t % 2], col[:, 0, :].unsqueeze(2).broadcast_to([P, KT, P]),
                                        ALU.mult).then_inc(s_fold, 1)
                dve.wait_ge(s_whi, 2 * t + 1)
                nc.vector.tensor_tensor(w1_lo[:, :, t * P:(t + 1) * P], stage1[t % 2],
                                        w1_hi[:, :, t * P:(t + 1) * P].bitcast(F32), ALU.subtract).then_inc(s_wlo, 1)
                dve.wait_ge(s_whi, 2 * t + 2)
                nc.vector.tensor_tensor(w2_lo[:, t, :], stage2[t % 2], w2_hi[:, t, :].bitcast(F32),
                                        ALU.subtract).then_inc(s_wlo, 1)

            def stats(g, n, par, b):
                if not (isinstance(n, int) and n < 2):
                    dve.wait_ge(s_ln, n - 1)
                dve.wait_ge(s_sum, n + 1)
                nc.vector.bn_stats(st[:, b % 2, :], n_row[par][:, b, :]).then_inc(s_bn, 1)
                wait_alone(dve, s_bn, n + 1)
                nc.vector.bn_aggr(mv[:, b % 2, :], st[:, b % 2, :]).then_inc(s_mv, 1)

            def add_residual(g, par, b):
                n = g * GB + b
                dve.wait_ge(s_down, g * (FT * GB) + ((FT - 1) * GB + b + 1))
                dve.wait_ge(s_res, n + 1)
                nc.vector.tensor_tensor(n_row[par][:, b, :], ps_down[b][:, :], n_row[par][:, b, :], ALU.add).then_inc(s_sum, 1)

            dve.wait_ge(s_const, 16 * 7)
            for b in range(GB):
                turn_lo(b, 0, b)
                if b < 2:
                    prep(b)

            def body(g, par, first, last):
                for step in ffn_steps(first, last, first):
                    if step[0] == "split":
                        t = step[1]
                        n = g * FT + t
                        dve.wait_ge(s_gelu, n + 1)
                        if not (first and t < 2):
                            dve.wait_ge(s_down, g * (FT * GB) + (t - 1) * GB)
                        nc.vector.tensor_copy(act_hi[t % 2][:, :], act_f[t % 2][:, :]).then_inc(s_act_hi, 1)
                        dve.wait_ge(s_act_hi, n + 1)
                        nc.vector.tensor_tensor(act_lo[t % 2][:, :], act_f[t % 2][:, :], act_hi[t % 2][:, :].bitcast(F32),
                                                ALU.subtract).then_inc(s_act, 1)
                    elif step[0] == "prep":
                        prep(step[1])
                    elif step[0] == "add_res":
                        add_residual(g - 1, 1 - par, step[1])
                    elif step[0] == "finish":
                        stats(g - 1, g * GB + (step[1] - GB), 1 - par, step[1])
                    elif step[0] == "turn":
                        turn_lo(g * GB + (GB + step[1]), 1 - par, step[1])
            run_pairs(dve, body)
            for b in range(GB):
                add_residual(ngroups - 1, 1, b)
            for b in range(GB):
                stats(ngroups - 1, (ngroups - 1) * GB + b, 1, b)

        @block.tensor
        def _(pe):
            def turn(n, g, par, b):
                pe.wait_ge(s_n2in[b], g * 16 + 16)
                wait(pe, s_turn_lo, n)
                for k in range(KT):
                    last = nc.tensor.transpose(ps_turn[:, k * P:(k + 1) * P], n_row[par][:, b, k * P:(k + 1) * P], ident[:, :])
                last.then_inc(s_turn, 1)

            def prep(t):
                pe.wait_ge(s_w1in[t % 2], 16 * (t // 2 + 1))
                wait(pe, s_bias, t)
                for k in range(KT):
                    last = nc.tensor.matmul(ps_vec[:, t:t + 1], stage1[t % 2][:, k, :], col[:, 1, k:k + 1],
                                            start=(k == 0), stop=(k == KT - 1))
                last.then_inc(s_matvec, 1)

            def down(g, t, first_group):
                pe.wait_ge(s_act, g * FT + (t + 1))
                if first_group:
                    pe.wait_ge(s_wlo, 2 * (t + 1))
                for b in range(GB):
                    if t == 0 and not first_group:
                        pe.wait_ge(s_sum, g * GB + (b + 1 - GB))
                    sl = slice(b * P, (b + 1) * P)
                    for i, (a, c) in enumerate(((act_hi, w2_hi), (act_hi, w2_lo), (act_lo, w2_hi))):
                        mm = nc.tensor.matmul(ps_down[b][:, :], a[t % 2][:, sl], c[:, t, :], start=(t == 0 and i == 0),
                                              stop=(t == FT - 1 and i == 2))
                    mm.then_inc(s_down, 1)

            pe.wait_ge(s_ident, 1)
            pe.wait_ge(s_const, 16 * 7)
            for b in range(GB):
                turn(b, 0, 0, b)
                if b < 2:
                    prep(b)

            def body(g, par, first, last):
                for step in ffn_steps(first, last, first):
                    if step[0] == "up":
                        t = step[1]
                        n = g * FT + t
                        if not (first and t < 2):
                            pe.wait_ge(s_gelu, n - 1)
                        if t == 0:
                            pe.wait_ge(s_turn_lo, g * GB + GB)
                        if first:
                            pe.wait_ge(s_wlo, 2 * t + 1)
                        for k in range(KT):
                            for i, (a, c) in enumerate(((w1_hi, nT_hi), (w1_hi, nT_lo), (w1_lo, nT_hi))):
                                mm = nc.tensor.matmul(ps_up[t % 2][:, :], a[:, k, t * P:(t + 1) * P], c[par][:, k, :],
                                                      start=(k == 0 and i == 0), stop=(k == KT - 1 and i == 2))
                        mm.then_inc(s_up, 1)
                    elif step[0] == "prep":
                        prep(step[1])
                    elif step[0] == "down":
                        if step[1] < 0:
                            down(g - 1, FT - 1, False)
                        else:
                            down(g, step[1], first)
                    elif step[0] == "turn":
                        turn(g * GB + (GB + step[1]), g + 1, 1 - par, step[1])
            run_pairs(pe, body)
            down(ngroups - 1, FT - 1, False)


def kernel(**inputs):
    import numpy as np
    import concourse.bacc as _bacc
    from concourse import mybir as _mybir
    from concourse.bass_utils import run_bass_kernel_spmd as _run

    pre = "L0_gnn_"

    def col(name):
        return np.asarray(inputs[pre + name]).reshape(-1, P).T

    arrays = {"x": np.ascontiguousarray(inputs["x"]), "adj": np.ascontiguousarray(inputs["adj"])}
    weights = (("q", "n2e_q"), ("k", "n2e_k"), ("v", "n2e_v"), ("q2", "e2n_q"), ("ek", "e2n_k"), ("ev", "e2n_v"))
    for short, name in weights:
        arrays[f"w_{short}"] = np.ascontiguousarray(np.asarray(inputs[f"{pre}{name}_w"]).T)
    for short in ("ffn_w1", "ffn_w2"):
        arrays[short] = np.ascontiguousarray(np.asarray(inputs[pre + short]).T)
    arrays["cols"] = np.ascontiguousarray(np.stack([col(n) for n in (
        "n2e_q_b", "n2e_k_b", "e2n_q_b", "e2n_k_b", "norm1_g", "norm1_b")], axis=1))
    arrays["cols_norm2"] = np.ascontiguousarray(np.stack([col("norm2_g"), col("norm2_b")], axis=1))
    arrays["cols_ffn_b1"] = np.ascontiguousarray(col("ffn_b1"))
    rows = ("n2e_v_b", "e2n_v_b", "norm2_g", "norm2_b", "ffn_b2", "norm3_g", "norm3_b")
    for name in rows:
        arrays[name] = np.ascontiguousarray(inputs[pre + name])
    nc = _bacc.Bacc("TRN2", target_bir_lowering=False, num_devices=1)
    ap = {n: nc.dram_tensor(f"in_{n}", a.shape, _mybir.dt.from_np(a.dtype), kind="ExternalInput").ap()
          for n, a in arrays.items()}
    shape = tuple(inputs["x"].shape)
    n2 = nc.dram_tensor("n2_scratch", shape, _mybir.dt.float32, kind="Internal").ap()
    out = nc.dram_tensor("out_0", shape, _mybir.dt.float32, kind="ExternalOutput").ap()
    attention_pass(nc, ap["x"], ap["adj"], {k: ap[f"w_{k}"] for k, _ in weights}, ap["cols"],
                   tuple(ap[n] for n in rows[:2]), n2)
    ffn_pass(nc, n2, ap["x"], ap["ffn_w1"], ap["ffn_w2"], (ap["cols_norm2"], ap["cols_ffn_b1"]),
             tuple(ap[n] for n in rows[2:]), out)
    r = _run(nc, [{f"in_{n}": a for n, a in arrays.items()}], core_ids=[0])
    return r.results[0]["out_0"]
```

```python
from contextlib import ExitStack

import concourse.bass as bass
from concourse import mybir

F32 = mybir.dt.float32
F32R = mybir.dt.float32r
BF16 = mybir.dt.bfloat16
ALU = mybir.AluOpType
ACT = mybir.ActivationFunctionType
AX = mybir.AxisListType

P = 128
D = 512
KT = D // P
H = 8
HD = D // H
HU = H // 2
HV = HD + 1
GB = 4
R = GB * P
DF = 2048
FT = DF // P
LN_EPS = 1e-5
SCALE = HD ** -0.5
MASKED = -1e30

UNITS = 4 * GB
TILES = 24
PRO_TILES = 12
TILE_KIND = ([("q2", 0), ("q2", 1), ("q2", 2), ("ev", 0), ("q2", 3), ("ev", 1), ("ev", 2)]
             + [("ek", m) for m in range(KT)] + [("ev", 3)]
             + [(w, m) for m in range(KT) for w in ("q", "k")] + [("v", b) for b in range(GB)])
TILE_OF = {k: t for t, k in enumerate(TILE_KIND)}
HALVES_L0 = (1,) * 8
HALVES_L1 = (3,) * 8
TRANSPOSES = 8


def steps_of_group(first, last):
    out = []

    def halves(lo, hi):
        for n in range(lo, hi):
            out.append(("half", n // 2, n % 2))
            if n % 2 == 1:
                out.append(("evac", n // 2))

    def tile(kind, idx):
        t = TILE_OF[(kind, idx)]
        halves(2 * t, 2 * t + 2)

    def finish(u):
        out.extend([("pt", u), ("pt_evac", u)])

    def values(u):
        out.extend([("av", u), ("norm", u), ("add_h", u)])

    for u in range(UNITS):
        layer, v = divmod(u, 8)
        out.extend([("scores", u), ("shift", u)])
        prev = u - 1 if u else -1
        has_prev = u not in (0, 8) or (u == 0 and not first)
        if v % 2 == 0:
            b = v // 2 - 2
            if b >= 0:
                out.append(("apply", layer, b))
            elif layer == 0 and not first:
                out.append(("apply", -1, b + 4))
        if has_prev:
            finish(prev)
        out.append(("exp", u))
        if v % 2 == 0:
            out.append(("h_again", layer, v // 2))
        if not last and u in (5, 7):
            out.append(("relu_x", (u - 5) // 2))
        if v in (3, 5, 7):
            out.append(("ln_row", layer, (v - 3) // 2))
        if u == 1 and not first:
            out.append(("ln_row", -1, 3))
        if u == 0 and not first:
            out.append(("mask", 0, 3))
        if u == 1 and not last:
            out.append(("load_adj",))
        if not last and u in (4, 6):
            out.append(("ln_x", (u - 4) // 2))
        if layer == 0:
            halves(sum(HALVES_L0[:v]), sum(HALVES_L0[:v + 1]))
        elif not last:
            halves(24 + sum(HALVES_L1[:v]), 24 + sum(HALVES_L1[:v + 1]))
        if has_prev:
            values(prev)
        if u == 0:
            out.append(("load_h", 0, 1))
            if not last:
                out.extend([("load_x", 0), ("load_x", 1)])
        if v >= 2 and v % 2 == 0:
            nb = v // 2 + 1
            if nb < GB:
                out.append(("load_h", layer, nb))
            elif layer == 0:
                out.append(("load_h", 1, 0))
            elif not last:
                out.append(("load_h", 2, 0))
        if not last and layer == 1 and v in (2, 4, 6):
            out.append(("mask", 1, v // 2 - 1))
        if not last and u == 15:
            out.append(("keep_stats",))
        if layer == 0 and v in (4, 6):
            out.extend([("t_edge", v // 2 - 2), ("t_evac", "edge", v // 2 - 2)])
        if u == 7:
            finish(7)
            out.append(("apply", 0, 2))
            halves(8, 9)
            values(7)
            halves(9, 10)
            out.append(("load_h", 1, 1))
            out.extend([("t_edge", 2), ("t_evac", "edge", 2), ("ln_row", 0, 3)])
            tile("ev", 1)
            if not last:
                out.extend([("t_h", 0), ("t_evac", "h", 0), ("load_x", 2)])
            out.append(("apply", 0, 3))
            halves(12, 13)
            out.extend([("t_edge", 3), ("t_evac", "edge", 3)])
            halves(13, 14)
            tile("ek", 0)
            if not last:
                out.extend([("t_h", 1), ("t_evac", "h", 1), ("load_x", 3), ("ln_x", 2), ("relu_x", 2)])
            tile("ek", 1)
            if not last:
                out.extend([("ln_x", 3), ("relu_x", 3)])
            tile("ek", 2)
            if not last:
                out.extend([("t_h", 2), ("t_evac", "h", 2)])
            tile("ek", 3)
            if not last:
                out.extend([("t_h", 3), ("t_evac", "h", 3)])
            tile("ev", 3)
    return out


def wait(eng, sem, value):
    if isinstance(value, int) and value <= 0:
        return
    eng.wait_ge(sem, value)


def wait_alone(eng, sem, value):
    if isinstance(value, int) and value <= 0:
        return
    eng.wait_ge(sem, value)
    eng.nop(nofuse=True)


def attention_pass(nc, x, adj, w, cols, rows_in, n2):
    ngroups = x.shape[0] // GB
    W_ORDER = ["q", "k", "v", "q2", "ek", "ev"]
    COL = {"q": 0, "k": 1, "q2": 2, "ek": 3, "g1": 4, "b1": 5}
    x_v = x.rearrange("(g b) p d -> g b p d", b=GB)
    n2_v = n2.rearrange("(g b) p d -> g b p d", b=GB)
    adj_v = adj.rearrange("(g b) i j -> g i b j", b=GB)

    def graph(view, g, b):
        if isinstance(g, int):
            return view[g, b]
        return view[bass.ds(g, 1), b].rearrange("o p d -> (o p) d")

    ctx = ExitStack()
    with ctx:
        def sb(name, shape, dt=F32):
            return ctx.enter_context(nc.sbuf_tensor(name, shape, dt))

        def sem(name):
            return ctx.enter_context(nc.semaphore(name))

        w_hi = {k: sb(f"w_{k}_hi", [P, KT, D], F32R) for k in W_ORDER}
        w_lo = {k: sb(f"w_{k}_lo", [P, KT, D], F32R) for k in W_ORDER}
        hT_hi, hT_lo = sb("hT_hi", [P, KT, R], F32R), sb("hT_lo", [P, KT, R], F32R)
        eT_hi, eT_lo = sb("eT_hi", [P, KT, R], F32R), sb("eT_lo", [P, KT, R], F32R)
        proj = {k: sb(f"proj_{k}", [P, KT, R]) for k in ("q", "k", "q2", "ek")}
        val = {k: sb(f"val_{k}", [P, GB, H, HV]) for k in ("v", "ev")}
        h_row = [sb(f"h_row{i}", [P, D]) for i in range(2)]
        x_row = [sb(f"x_row{i}", [P, D]) for i in range(2)]
        row = [sb(f"row{i}", [P, D]) for i in range(GB)]
        prob = [sb(f"prob{i}", [P, HU * P]) for i in range(2)]
        probT = sb("probT", [P, HU * P])
        bias_row = {"v": sb("bias_v", [P, D]), "ev": sb("bias_ev", [P, D])}
        col = sb("col", [P, 6, KT])
        adj_in = sb("adj_in", [P, GB, P])
        mask = sb("mask", [P, GB, P], BF16)
        ident = sb("ident", [P, P])
        ident_b = sb("ident_b", [P, P], BF16)
        neg_half = sb("neg_half", [P, 1])
        peak = sb("peak", [P, 2, HU])
        recip = sb("recip", [P, 2, HU])
        st_row, st_x = sb("st_row", [P, GB, 6]), sb("st_x", [P, 2, 6])
        mv_row, mv_x = sb("mv_row", [P, GB, 2]), sb("mv_x", [P, 2, 2])
        var_row, var_x = sb("var_row", [P, 1]), sb("var_x", [P, 1])
        ln_row = sb("ln_row", [P, GB, 2])
        ln_next, ln_cur = sb("ln_next", [P, GB, 2]), sb("ln_cur", [P, GB, 2])

        bank = [ctx.enter_context(nc.psum_tensor(f"bank{i}", [P, 512], F32)) for i in range(8)]
        ps_scores, ps_tile, ps_av = bank[0:2], bank[2:4], bank[4:6]
        ps_probT, ps_turn = bank[6], bank[7]

        s_const = sem("s_const")
        s_ident0, s_ident = sem("s_ident0"), sem("s_ident")
        s_ones = sem("s_ones")
        s_stage = [sem(f"s_stage{i}") for i in range(2)]
        s_matvec = sem("s_matvec")
        s_bias = sem("s_bias")
        s_fold = sem("s_fold")
        s_whi, s_wlo = sem("s_whi"), sem("s_wlo")
        s_adj = sem("s_adj")
        s_mask = sem("s_mask")
        s_xin = [sem(f"s_xin{i}") for i in range(2)]
        s_xfirst = [sem(f"s_xfirst{i}") for i in range(2)]
        s_hin = [sem(f"s_hin{i}") for i in range(2)]
        s_hagain = sem("s_hagain")
        s_scores, s_peak, s_shift, s_exp = sem("s_scores"), sem("s_peak"), sem("s_shift"), sem("s_exp")
        s_pt, s_pt_evac = sem("s_pt"), sem("s_pt_evac")
        s_av, s_recip, s_norm, s_add = sem("s_av"), sem("s_recip"), sem("s_norm"), sem("s_add")
        s_tile = sem("s_tile")
        s_evac = [sem(f"s_evac{i}") for i in range(2)]
        s_turn, s_turn_hi, s_turn_lo = sem("s_turn"), sem("s_turn_hi"), sem("s_turn_lo")
        s_bn_row, s_mv_row, s_var_row, s_rstd_row, s_ln_row = (sem(f"s_{n}_row") for n in ("bn", "mv", "var", "rstd", "ln"))
        s_bn_x, s_mv_x, s_var_x, s_rstd_x, s_ln_x = (sem(f"s_{n}_x") for n in ("bn", "mv", "var", "rstd", "ln"))
        s_apply, s_relu, s_keep = sem("s_apply"), sem("s_relu"), sem("s_keep")
        s_store = [sem(f"s_store{i}") for i in range(GB)]

        def turn_no(g, kind, b):
            order = {"edge": (0, 1, 2, 4), "h": (3, 5, 6, 7)}[kind]
            if isinstance(g, int) and g == ngroups - 1:
                order = range(GB)
            return GB + TRANSPOSES * g + order[b]

        def wait_tile(eng, g, t):
            wait(eng, s_evac[t % 2], (PRO_TILES + TILES * g) // 2 + t // 2 + 1 if isinstance(g, int)
                 else g * (TILES // 2) + (PRO_TILES // 2 + t // 2 + 1))

        def parity_heads(ap, par):
            return ap.rearrange("p (j two d) -> p two j d", two=2, d=HD)[:, par]

        def run_groups(eng, body):
            body(0, True, False)
            with eng.Fori(1, ngroups - 1) as g:
                body(g, False, False)
            body(ngroups - 1, False, True)

        block = ctx.enter_context(nc.Block())

        @block.sync
        def _(sp):
            def load_x(g, b):
                sp.dma_start(x_row[b % 2][:, :], graph(x_v, g, b)).then_inc(s_xin[b % 2], 16)

            def load_h(g, b):
                sp.dma_start(h_row[b % 2][:, :], graph(x_v, g, b)).then_inc(s_hin[b % 2], 16)

            def load_adj(g):
                src = adj_v[g] if isinstance(g, int) else adj_v[bass.ds(g, 1)].rearrange("o i b j -> (o i) b j")
                sp.dma_start(adj_in[:, :, :], src).then_inc(s_adj, 16)

            def store_n2(g, b):
                wait_alone(sp, s_store[(b - 1) % GB], (g + (1 if b else 0)) * 16)
                sp.dma_start(graph(n2_v, g, b), row[b][:, :]).then_inc(s_store[b], 16)

            load_x(0, 0)
            load_x(0, 1)
            for b in (2, 3):
                sp.dma_start(h_row[b % 2][:, :], graph(x_v, 0, b)).then_inc(s_xfirst[b % 2], 16)
            stage = (proj["q2"], proj["ek"])
            for i, k in enumerate(W_ORDER):
                if i >= 2:
                    sp.wait_ge(s_wlo, i - 1)
                sp.dma_start(stage[i % 2][:, :, :], w[k].rearrange("(k p) n -> p k n", p=P)).then_inc(s_stage[i % 2], 16)
                if i == 1:
                    sp.dma_start(col[:, :, :], cols).then_inc(s_const, 16)
                    for kk, src in zip(("v", "ev"), rows_in):
                        sp.dma_start(bias_row[kk][:, :], src.partition_broadcast(P)).then_inc(s_const, 16)
                    load_adj(0)
            sp.wait_ge(s_turn, 4)
            load_h(0, 0)

            def body(g, first, last):
                for step in steps_of_group(first, last):
                    if step[0] == "load_x":
                        b = step[1]
                        if b < 2:
                            wait_alone(sp, s_turn, 4 if first else turn_no(g - 1, "h", b + 2) + 1)
                        else:
                            wait_alone(sp, s_turn, turn_no(g, "h", b - 2) + 1)
                        load_x(g + 1, b)
                    elif step[0] == "load_h":
                        layer, b = step[1:]
                        unit = 8 * layer + 2 * b - 3
                        wait_alone(sp, s_add, g * UNITS + unit + 1 if not (first and unit < 0) else 0)
                        load_h(g + 1 if layer == 2 else g, b)
                    elif step[0] == "load_adj":
                        wait_alone(sp, s_mask, g * GB + GB)
                        load_adj(g + 1)
                    elif step[0] == "apply" and step[1] != 0:
                        gg, b = (g if step[1] == 1 else g - 1), step[2]
                        wait_alone(sp, s_apply, gg * 8 + 4 + b + 1)
                        store_n2(gg, b)
            run_groups(sp, body)
            for b in (2, 3):
                sp.wait_ge(s_apply, 8 * (ngroups - 1) + 4 + b + 1)
                store_n2(ngroups - 1, b)
            for b in range(GB):
                sp.wait_ge(s_store[b], 16 * ngroups)

        @block.gpsimd
        def _(pool):
            nc.gpsimd.memset(ident[:, :], 0.0).then_inc(s_ident0, 1)
            nc.gpsimd.memset(ident_b[:, :], 0.0).then_inc(s_ident0, 1)
            nc.gpsimd.memset(neg_half[:, :], -0.5).then_inc(s_ident0, 1)
            pool.wait_ge(s_ident0, 3)
            for m in (ident, ident_b):
                nc.gpsimd.affine_select(out=m[:, :], in_=m[:, :], compare_op=ALU.not_equal, fill=1.0,
                                        base=0, pattern=[[-1, P]], channel_multiplier=1).then_inc(s_ident, 1)

            def make_mask(g, b):
                wait_alone(pool, s_adj, g * 16 + 16)
                nc.gpsimd.tensor_scalar(mask[:, b, :], adj_in[:, b, :], 0.0, MASKED, ALU.is_le, ALU.mult).then_inc(s_mask, 1)

            def norm_factors(n, mv, var, rstd, shift, s_mv, s_var, s_rstd, s_ln):
                wait_alone(pool, s_mv, n + 1)
                nc.gpsimd.tensor_scalar(var[:, :], mv[:, 1:2], LN_EPS, None, ALU.add).then_inc(s_var, 1)
                pool.wait_ge(s_var, n + 1)
                nc.gpsimd.tensor_tensor(rstd, var[:, :], neg_half[:, :], ALU.pow).then_inc(s_rstd, 1)
                wait_alone(pool, s_rstd, n + 1)
                nc.gpsimd.tensor_scalar(shift, mv[:, 0:1], rstd, -1.0, ALU.mult, ALU.mult).then_inc(s_ln, 1)

            def ln_x(n, b):
                norm_factors(n, mv_x[:, b % 2, :], var_x, ln_next[:, b, 0:1], ln_next[:, b, 1:2],
                             s_mv_x, s_var_x, s_rstd_x, s_ln_x)

            def ln_rows(n, b):
                if not (isinstance(n, int) and n < 2):
                    wait_alone(pool, s_apply, n - 1)
                norm_factors(n, mv_row[:, b, :], var_row, ln_row[:, b, 0:1], ln_row[:, b, 1:2],
                             s_mv_row, s_var_row, s_rstd_row, s_ln_row)

            for b in range(GB):
                ln_x(b, b)
            for b in range(GB):
                make_mask(0, b)

            def body(g, first, last):
                for step in steps_of_group(first, last):
                    if step[0] == "mask":
                        b = step[2]
                        gg = g + step[1]
                        wait_alone(pool, s_scores, (gg - 1) * UNITS + 8 + 2 * b + 2)
                        make_mask(gg, b)
                    elif step[0] == "ln_x":
                        b = step[1]
                        wait_alone(pool, s_keep, g + 1)
                        ln_x(g * GB + (GB + b), b)
                    elif step[0] == "ln_row":
                        ln_rows(g * 8 + 4 * step[1] + step[2], step[2])
                    elif step[0] == "add_h":
                        u = step[1]
                        b, par = (u % 8) // 2, u % 2
                        n = g * UNITS + u
                        pool.wait_ge(s_norm, n + 1)
                        pool.wait_ge(s_hagain, g * 8 + u // 2 + 1)
                        out = parity_heads(row[b][:, :], par)
                        nc.gpsimd.tensor_tensor(out, out, parity_heads(h_row[b % 2][:, :], par), ALU.add).then_inc(s_add, 1)
            run_groups(pool, body)
            n = ngroups * UNITS - 1
            pool.wait_ge(s_norm, n + 1)
            out = parity_heads(row[3][:, :], 1)
            nc.gpsimd.tensor_tensor(out, out, parity_heads(h_row[1][:, :], 1), ALU.add).then_inc(s_add, 1)
            ln_rows(ngroups * 8 - 1, 3)

        @block.scalar
        def _(act):
            def relu_x(n, b, rows=x_row):
                act.wait_ge(s_ln_x, n + 1)
                nc.scalar.activation(rows[b % 2][:, :], rows[b % 2][:, :], ACT.Relu, bias=ln_next[:, b, 1:2],
                                     scale=ln_next[:, b, 0:1]).then_inc(s_relu, 1)

            def turn_hi(no, kind, b):
                dst = hT_hi if kind == "h" else eT_hi
                wait(act, s_turn, no + 1)
                nc.scalar.activation(dst[:, :, b * P:(b + 1) * P], ps_turn[:, :].rearrange("p (k r) -> p k r", k=KT),
                                     ACT.Copy).then_inc(s_turn_hi, 1)

            def split_hi(i):
                if i < 4:
                    act.wait_ge(s_stage[i % 2], 16 * (i // 2 + 1))
                else:
                    act.wait_ge(s_fold, i - 3)
                nc.scalar.activation(w_hi[W_ORDER[i]][:, :, :], (proj["q2"], proj["ek"])[i % 2][:, :, :],
                                     ACT.Copy).then_inc(s_whi, 1)

            def evac(no, t):
                kind, m = TILE_KIND[t]
                if kind in ("v", "ev"):
                    return
                wait(act, s_tile, no + 1)
                nc.scalar.activation(proj[kind][:, m, :], ps_tile[t % 2][:, :], ACT.Identity,
                                     bias=col[:, COL[kind], m:m + 1]).then_inc(s_evac[t % 2], 1)

            def keep():
                nc.scalar.activation(ln_cur[:, :, :], ln_next[:, :, :], ACT.Copy).then_inc(s_keep, 1)

            def apply(n, b):
                act.wait_ge(s_ln_row, n + 1)
                nc.scalar.activation(row[b][:, :], row[b][:, :], ACT.Identity, bias=ln_row[:, b, 1:2],
                                     scale=ln_row[:, b, 0:1]).then_inc(s_apply, 1)

            for b in range(GB):
                relu_x(b, b, x_row if b < 2 else h_row)
                if b:
                    turn_hi(b - 1, "h", b - 1)
            turn_hi(GB - 1, "h", GB - 1)
            split_hi(0)
            split_hi(1)
            keep()
            act.wait_ge(s_const, 48)
            for t in range(TILES - PRO_TILES, TILES):
                evac(t - PRO_TILES, t)
                if t - (TILES - PRO_TILES) in (1, 3):
                    split_hi((t - (TILES - PRO_TILES)) // 2 + 2)
            split_hi(4)
            split_hi(5)

            def pt_evac(n, u):
                act.wait_ge(s_pt, n + 1)
                nc.scalar.activation(probT[:, :], ps_probT[:, :], ACT.Copy).then_inc(s_pt_evac, 1)

            def body(g, first, last):
                for step in steps_of_group(first, last):
                    if step[0] == "pt_evac":
                        pt_evac(g * UNITS + step[1], step[1] % UNITS)
                    elif step[0] == "h_again":
                        layer, b = step[1:]
                        act.wait_ge(s_hin[b % 2], g * 64 + 16 * (2 * layer + b // 2 + 1))
                        act.wait_ge(s_keep, g + 1)
                        nc.scalar.activation(h_row[b % 2][:, :], h_row[b % 2][:, :], ACT.Relu, bias=ln_cur[:, b, 1:2],
                                             scale=ln_cur[:, b, 0:1]).then_inc(s_hagain, 1)
                    elif step[0] == "exp":
                        u = step[1]
                        act.wait_ge(s_shift, g * UNITS + u + 1)
                        nc.scalar.activation(prob[u % 2][:, :], prob[u % 2][:, :], ACT.Exp, scale=SCALE).then_inc(s_exp, 1)
                    elif step[0] == "evac":
                        evac(g * TILES + (PRO_TILES + step[1]), step[1])
                    elif step[0] == "apply":
                        apply(g * 8 + 4 * step[1] + step[2], step[2])
                    elif step[0] == "relu_x":
                        relu_x(g * GB + (GB + step[1]), step[1])
                    elif step[0] == "t_evac":
                        turn_hi(turn_no(g, step[1], step[2]), step[1], step[2])
                    elif step[0] == "keep_stats":
                        act.wait_ge(s_hagain, g * 8 + 8)
                        keep()
            run_groups(act, body)
            apply(ngroups * 8 - 2, 2)
            pt_evac(ngroups * UNITS - 1, UNITS - 1)
            apply(ngroups * 8 - 1, 3)

        @block.vector
        def _(dve):
            for k in ("v", "ev"):
                last_ones = nc.vector.memset(val[k][:, :, :, HD:HV], 1.0).then_inc(s_ones, 1)

            def stats(n, src, st, mv, s_bn, s_mv):
                nc.vector.bn_stats(st, src).then_inc(s_bn, 1)
                wait_alone(dve, s_bn, n + 1)
                nc.vector.bn_aggr(mv, st).then_inc(s_mv, 1)

            def ln_x(g, n, b, rows=x_row):
                if rows is h_row:
                    dve.wait_ge(s_xfirst[b % 2], 16)
                else:
                    dve.wait_ge(s_xin[b % 2], g * 32 + 16 * (b // 2 + (1 if isinstance(g, int) and g == 0 else 0)))
                if not (isinstance(n, int) and n < 2):
                    dve.wait_ge(s_ln_x, n - 1)
                stats(n, rows[b % 2][:, :], st_x[:, b % 2, :], mv_x[:, b % 2, :], s_bn_x, s_mv_x)

            def ln_rows(n, b, unit_no):
                dve.wait_ge(s_add, unit_no + 1)
                stats(n, row[b][:, :], st_row[:, b, :], mv_row[:, b, :], s_bn_row, s_mv_row)

            def turn_lo(no, kind, b):
                hi, lo = (hT_hi, hT_lo) if kind == "h" else (eT_hi, eT_lo)
                dve.wait_ge(s_turn_hi, no + 1)
                nc.vector.tensor_tensor(lo[:, :, b * P:(b + 1) * P], ps_turn[:, :].rearrange("p (k r) -> p k r", k=KT),
                                        hi[:, :, b * P:(b + 1) * P].bitcast(F32), ALU.subtract).then_inc(s_turn_lo, 1)

            def split_lo(i):
                k = W_ORDER[i]
                stage = (proj["q2"], proj["ek"])[i % 2]
                if i >= 4:
                    dve.wait_ge(s_stage[i % 2], 16 * (i // 2 + 1))
                    dve.wait_ge(s_matvec, i - 3)
                    if k == "ek":
                        nc.vector.tensor_tensor(col[:, COL["ek"], :], ps_av[0][:, 0:KT], col[:, COL["ek"], :],
                                                ALU.add).then_inc(s_bias, 1)
                    else:
                        nc.vector.tensor_tensor(bias_row["ev"][:, :], ps_av[1][:, :], bias_row["ev"][:, :],
                                                ALU.add).then_inc(s_bias, 1)
                    for t in range(KT):
                        folded = nc.vector.tensor_scalar(stage[:, t, :], stage[:, t, :], col[:, COL["g1"], t:t + 1],
                                                         None, ALU.mult)
                    folded.then_inc(s_fold, 1)
                dve.wait_ge(s_whi, i + 1)
                nc.vector.tensor_tensor(w_lo[k][:, :, :], stage[:, :, :], w_hi[k][:, :, :].bitcast(F32),
                                        ALU.subtract).then_inc(s_wlo, 1)

            def evac(no, t):
                kind, b = TILE_KIND[t]
                if kind not in ("v", "ev"):
                    return
                wait(dve, s_tile, no + 1)
                nc.vector.tensor_tensor(val[kind][:, b, :, 0:HD], ps_tile[t % 2][:, :].rearrange("p (h d) -> p h d", h=H),
                                        bias_row[kind][:, :].rearrange("p (h d) -> p h d", h=H),
                                        ALU.add).then_inc(s_evac[t % 2], 1)

            for b in range(GB):
                ln_x(0, b, b, x_row if b < 2 else h_row)
            for b in range(GB):
                turn_lo(b, "h", b)
            for i in range(4):
                split_lo(i)
            dve.wait_ge(s_const, 48)
            split_lo(4)
            for b in range(GB):
                evac(8 + b, TILE_OF[("v", b)])
                if b == 1:
                    split_lo(5)
            dve.wait_ge(s_bias, 2)

            def normalise(g, n, u):
                layer, b, par = (u % UNITS) // 8, (u % 8) // 2, u % 2
                dve.wait_ge(s_av, n + 1)
                src = ps_av[par][:, 0:HU * HV].rearrange("p (j d) -> p j d", d=HV)
                nc.vector.reciprocal(recip[:, par, :], src[:, :, HD]).then_inc(s_recip, 1)
                if par == 0 and layer == 0:
                    wait(dve, s_store[b], g * 16)
                elif par == 0:
                    dve.wait_ge(s_turn, turn_no(g, "edge", b) + 1)
                dve.wait_ge(s_recip, n + 1)
                nc.vector.tensor_tensor(parity_heads(row[b][:, :], par), src[:, :, 0:HD],
                                        recip[:, par, :].unsqueeze(2).broadcast_to([P, HU, HD]), ALU.mult).then_inc(s_norm, 1)

            def body(g, first, last):
                for step in steps_of_group(first, last):
                    if step[0] == "shift":
                        u = step[1]
                        n = g * UNITS + u
                        src = ps_scores[u % 2][:, :].rearrange("p (j k) -> p j k", j=HU)
                        dve.wait_ge(s_scores, n + 1)
                        nc.vector.tensor_reduce(peak[:, u % 2, :], src, AX.X, ALU.max).then_inc(s_peak, 1)
                        if not (first and u < 2):
                            dve.wait_ge(s_pt, n - 1)
                        dve.wait_ge(s_peak, n + 1)
                        nc.vector.tensor_tensor(prob[u % 2][:, :].rearrange("p (j k) -> p j k", j=HU), src,
                                                peak[:, u % 2, :].unsqueeze(2).broadcast_to([P, HU, P]),
                                                ALU.subtract).then_inc(s_shift, 1)
                    elif step[0] == "norm":
                        normalise(g, g * UNITS + step[1], step[1])
                    elif step[0] == "evac":
                        evac(g * TILES + (PRO_TILES + step[1]), step[1])
                    elif step[0] == "ln_row":
                        layer, b = step[1:]
                        ln_rows(g * 8 + 4 * layer + b, b, g * UNITS + 8 * layer + 2 * b + 1)
                    elif step[0] == "ln_x":
                        ln_x(g + 1, g * GB + (GB + step[1]), step[1])
                    elif step[0] == "t_evac":
                        turn_lo(turn_no(g, step[1], step[2]), step[1], step[2])
            run_groups(dve, body)
            normalise(ngroups, ngroups * UNITS - 1, -1)
            ln_rows(ngroups * 8 - 1, 3, ngroups * UNITS - 1)

        @block.tensor
        def _(pe):
            def turn(no, src, ready, count):
                wait(pe, ready, count)
                wait(pe, s_turn_lo, no)
                for k in range(KT):
                    last = nc.tensor.transpose(ps_turn[:, k * P:(k + 1) * P], src[:, k * P:(k + 1) * P], ident[:, :])
                last.then_inc(s_turn, 1)

            def half_tile(g, t, part):
                kind, m = TILE_KIND[t]
                hi, lo = (eT_hi, eT_lo) if kind in ("ek", "ev") else (hT_hi, hT_lo)
                if part == 0:
                    wait(pe, s_evac[t % 2], g * (TILES // 2) + (PRO_TILES // 2 + t // 2))
                for k in range(2 * part, 2 * part + 2):
                    for a, c in (("hi", "hi"), ("hi", "lo"), ("lo", "hi")):
                        if kind in ("v", "ev"):
                            lhsT = (hi if a == "hi" else lo)[:, k, m * P:(m + 1) * P]
                            rhs = (w_hi if c == "hi" else w_lo)[kind][:, k, :]
                        else:
                            lhsT = (w_hi if a == "hi" else w_lo)[kind][:, k, m * P:(m + 1) * P]
                            rhs = (hi if c == "hi" else lo)[:, k, :]
                        last = nc.tensor.matmul(ps_tile[t % 2][:, :], lhsT, rhs, start=(k == 0 and a + c == "hihi"),
                                                stop=(k == KT - 1 and a == "lo"))
                if part == 1:
                    last.then_inc(s_tile, 1)

            pe.wait_ge(s_ident, 2)
            for b in range(GB):
                turn(b, (x_row if b < 2 else h_row)[b % 2], s_relu, b + 1)
            pe.wait_ge(s_turn_lo, GB)

            def first_tiles(kinds):
                for t in range(TILES - PRO_TILES, TILES):
                    if TILE_KIND[t] in kinds:
                        pe.wait_ge(s_wlo, {"q": 1, "k": 2, "v": 3}[TILE_KIND[t][0]])
                        half_tile(-1, t, 0)
                        half_tile(-1, t, 1)

            first_tiles([(w_, m) for w_ in ("q", "k") for m in range(KT)])
            pe.wait_ge(s_const, 48)
            pe.wait_ge(s_stage[0], 48)
            for m in range(KT):
                for k in range(KT):
                    last = nc.tensor.matmul(ps_av[0][:, m:m + 1], proj["q2"][:, k, m * P:(m + 1) * P],
                                            col[:, COL["b1"], k:k + 1], start=(k == 0), stop=(k == KT - 1))
            last.then_inc(s_matvec, 1)
            first_tiles([("v", 0), ("v", 1)])
            pe.wait_ge(s_stage[1], 48)
            for k in range(KT):
                last = nc.tensor.matmul(ps_av[1][:, :], col[:, COL["b1"], k:k + 1].broadcast_to([P, P]),
                                        proj["ek"][:, k, :], start=(k == 0), stop=(k == KT - 1))
            last.then_inc(s_matvec, 1)
            first_tiles([("v", 2), ("v", 3)])
            pe.wait_ge(s_wlo, 6)
            pe.wait_ge(s_bias, 2)
            pe.wait_ge(s_ones, 2)

            def transpose_probs(n, u):
                pe.wait_ge(s_exp, n + 1)
                wait(pe, s_pt_evac, n)
                for j in range(HU):
                    last = nc.tensor.transpose(ps_probT[:, j * P:(j + 1) * P], prob[u % 2][:, j * P:(j + 1) * P], ident[:, :])
                last.then_inc(s_pt, 1)

            def attend(g, n, u):
                layer, b, par = (u % UNITS) // 8, (u % 8) // 2, u % 2
                pe.wait_ge(s_pt_evac, n + 1)
                wait(pe, s_norm, n - 1)
                if layer == 0 and u % UNITS < 2:
                    wait_tile(pe, g - 1, TILE_OF[("v", 2)])
                    wait_tile(pe, g - 1, TILE_OF[("v", 3)])
                elif layer == 1 and par == 0:
                    wait_tile(pe, g, TILE_OF[("ev", b)])
                for j in range(HU):
                    last = nc.tensor.matmul(ps_av[par][:, j * HV:(j + 1) * HV], probT[:, j * P:(j + 1) * P],
                                            val[("v", "ev")[layer]][:, b, 2 * j + par, :], start=True, stop=True)
                last.then_inc(s_av, 1)

            def body(g, first, last):
                for step in steps_of_group(first, last):
                    if step[0] == "scores":
                        u = step[1]
                        layer, b, par = u // 8, (u % 8) // 2, u % 2
                        n = g * UNITS + u
                        if not (first and u < 2):
                            pe.wait_ge(s_shift, n - 1)
                        if layer == 0 and par == 0:
                            pe.wait_ge(s_mask, g * GB + (b + 1))
                        if layer == 0 and u == 0:
                            wait_tile(pe, g - 1, TILE_OF[("q", 3)])
                            wait_tile(pe, g - 1, TILE_OF[("k", 3)])
                        if layer == 1 and u == 8:
                            wait_tile(pe, g, TILE_OF[("ek", 3)])
                            wait_tile(pe, g, TILE_OF[("ek", 2)])
                        every = (lambda ap: ap.unsqueeze(1).broadcast_to([P, HU, P]))
                        out = ps_scores[u % 2]
                        if layer == 0:
                            nc.tensor.matmul(out[:, :], mask[:, b, :], every(ident_b[:, :]), start=True, stop=False)
                        else:
                            nc.tensor.matmul(out[:, :], ident_b[:, :], every(mask[:, b, :]), start=True, stop=False)
                        q, k = (proj["q"], proj["k"]) if layer == 0 else (proj["q2"], proj["ek"])
                        half = slice(HD * par, HD * (par + 1))
                        for j in range(HU):
                            mm = nc.tensor.matmul(out[:, j * P:(j + 1) * P], q[half, j, b * P:(b + 1) * P],
                                                  k[half, j, b * P:(b + 1) * P], start=False, stop=(j == HU - 1))
                        mm.then_inc(s_scores, 1)
                    elif step[0] == "pt":
                        transpose_probs(g * UNITS + step[1], step[1] % UNITS)
                    elif step[0] == "av":
                        attend(g, g * UNITS + step[1], step[1] % UNITS)
                    elif step[0] == "half":
                        t, part = step[1:]
                        if part == 0 and TILE_KIND[t][0] in ("ev", "ek", "q"):
                            kind, m = TILE_KIND[t]
                            turned = ("edge", m) if kind == "ev" else ("edge", 3) if kind == "ek" else ("h", 3)
                            pe.wait_ge(s_turn_lo, turn_no(g, *turned) + 1)
                        half_tile(g, t, part)
                    elif step[0] == "t_edge":
                        b = step[1]
                        turn(turn_no(g, "edge", b), row[b], s_apply, g * 8 + (b + 1))
                    elif step[0] == "t_h":
                        b = step[1]
                        turn(turn_no(g, "h", b), x_row[b % 2], s_relu, g * GB + (GB + b + 1))
            run_groups(pe, body)
            transpose_probs(ngroups * UNITS - 1, UNITS - 1)
            attend(ngroups - 1, ngroups * UNITS - 1, UNITS - 1)


def ffn_steps(g_first, g_last, prep):
    out = []
    for t in range(FT):
        out.extend([("up", t), ("gelu", t)])
        if prep and t + 2 < FT:
            out.extend([("prep", t + 2)])
        if t or not g_first:
            out.append(("down", t - 1))
        out.append(("split", t))
        if t == 0 and not g_first:
            out.extend([("add_res", mt) for mt in range(GB)])
        if 1 <= t <= GB and not g_first:
            out.append(("finish", t - 1))
        if 2 <= t <= GB + 1 and not g_first:
            out.append(("gain", t - 2))
        if 5 <= t < 5 + GB and not g_last and not g_first:
            out.append(("load_n2", t - 5))
        if 7 <= t < 7 + GB:
            out.append(("load_x", t - 7))
        if 11 <= t < 11 + GB:
            out.append(("shift_x", t - 11))
        if t == FT - 2 and g_first and not g_last:
            out.extend([("load_n2", b) for b in range(GB)])
        if not g_last:
            at = (8, 10, 12, 14) if not g_first else (15, 15, 15, 15)
            out.extend([("turn", b) for b in range(GB) if at[b] == t])
    return out


def ffn_pass(nc, n2, x, w1, w2, cols, rows_in, out):
    cols_n, cols_b = cols
    ngroups = x.shape[0] // GB
    x_v = x.rearrange("(g b) p d -> g b p d", b=GB)
    n2_v = n2.rearrange("(g b) p d -> g b p d", b=GB)
    out_v = out.rearrange("(g b) p d -> g b p d", b=GB)
    w1_v = w1.rearrange("(k p) (t n) -> t p k n", p=P, n=P)
    w2_v = w2.rearrange("(t p) n -> t p n", p=P)

    def graph(view, g, b):
        if isinstance(g, int):
            return view[g, b]
        return view[bass.ds(g, 1), b].rearrange("o p d -> (o p) d")

    ctx = ExitStack()
    with ctx:
        def sb(name, shape, dt=F32):
            return ctx.enter_context(nc.sbuf_tensor(name, shape, dt))

        def sem(name):
            return ctx.enter_context(nc.semaphore(name))

        w1_hi, w1_lo = sb("w1_hi", [P, KT, DF], F32R), sb("w1_lo", [P, KT, DF], F32R)
        w2_hi, w2_lo = sb("w2_hi", [P, FT, D], F32R), sb("w2_lo", [P, FT, D], F32R)
        nT_hi = [sb(f"nT_hi{i}", [P, KT, R], F32R) for i in range(2)]
        nT_lo = [sb(f"nT_lo{i}", [P, KT, R], F32R) for i in range(2)]
        n_row = [sb(f"n_row{i}", [P, GB, D]) for i in range(2)]
        x_res = [sb(f"x_res{i}", [P, D]) for i in range(GB)]
        act_f = [sb(f"act_f{i}", [P, R]) for i in range(2)]
        act_hi = [sb(f"act_hi{i}", [P, R], F32R) for i in range(2)]
        act_lo = [sb(f"act_lo{i}", [P, R], F32R) for i in range(2)]
        gain2, shift2 = sb("gain2", [P, D]), sb("shift2", [P, D])
        gain3, shift3 = sb("gain3", [P, D]), sb("shift3", [P, D])
        bias_down = act_f[1]
        col = sb("fcol", [P, 2, KT])
        bias_up = sb("bias_up", [P, FT])
        ident = sb("fident", [P, P])
        neg_half = sb("fneg_half", [P, 1])
        st = sb("fst", [P, 2, 6])
        mv = sb("fmv", [P, 2, 2])
        var = sb("fvar", [P, 1])
        ln = sb("fln", [P, 2, 2])

        bank = [ctx.enter_context(nc.psum_tensor(f"fbank{i}", [P, 512], F32)) for i in range(8)]
        ps_up, ps_down, ps_turn, ps_vec = bank[0:2], bank[2:6], bank[6], bank[7]

        s_const = sem("f_const")
        s_ident0, s_ident = sem("f_ident0"), sem("f_ident")
        s_shift2 = sem("f_shift2")
        s_w1in = [sem(f"f_w1in{i}") for i in range(2)]
        s_w2in = [sem(f"f_w2in{i}") for i in range(2)]
        s_matvec, s_bias, s_fold = sem("f_matvec"), sem("f_bias"), sem("f_fold")
        s_whi, s_wlo = sem("f_whi"), sem("f_wlo")
        s_n2in = [sem(f"f_n2in{b}") for b in range(GB)]
        s_xin = [sem(f"f_xin{i}") for i in range(GB)]
        s_turn, s_turn_hi, s_turn_lo = sem("f_turn"), sem("f_turn_hi"), sem("f_turn_lo")
        s_gain, s_res = sem("f_gain"), sem("f_res")
        s_up, s_gelu, s_act_hi, s_act = sem("f_up"), sem("f_gelu"), sem("f_act_hi"), sem("f_act")
        s_down = sem("f_down")
        s_sum = sem("f_sum")
        s_bn, s_mv, s_var, s_rstd, s_ln = (sem(f"f_{n}") for n in ("bn", "mv", "var", "rstd", "ln"))
        s_apply, s_gain3, s_xb, s_out = sem("f_apply"), sem("f_gain3"), sem("f_xb"), sem("f_out")
        s_store = [sem(f"f_store{b}") for b in range(GB)]

        stage1 = [n_row[1][:, 2 * i, :].rearrange("p (k n) -> p k n", k=KT) for i in range(2)]
        stage2 = [n_row[1][:, 2 * i + 1, :] for i in range(2)]

        def run_pairs(eng, body):
            body(0, 0, True, False)
            body(1, 1, False, False)
            with eng.Fori(1, ngroups // 2 - 1) as pair:
                body(pair * 2, 0, False, False)
                body(pair * 2 + 1, 1, False, False)
            body(ngroups - 2, 0, False, False)
            body(ngroups - 1, 1, False, True)

        block = ctx.enter_context(nc.Block())

        @block.sync
        def _(sp):
            def load_n2(g, par, b):
                sp.dma_start(n_row[par][:, b, :], graph(n2_v, g, b)).then_inc(s_n2in[b], 16)

            def load_x(g, b):
                sp.dma_start(x_res[b][:, :], graph(x_v, g, b)).then_inc(s_xin[b], 16)

            def load_weights(t):
                if t >= 2:
                    sp.wait_ge(s_wlo, 2 * (t - 1))
                sp.dma_start(stage1[t % 2], w1_v[t]).then_inc(s_w1in[t % 2], 16)
                sp.dma_start(stage2[t % 2], w2_v[t]).then_inc(s_w2in[t % 2], 16)

            def store(g, par, b):
                wait_alone(sp, s_out, g * GB + (b + 1))
                sp.dma_start(graph(out_v, g, b), n_row[par][:, b, :]).then_inc(s_store[b], 16)

            for b in range(GB):
                load_n2(0, 0, b)
                if b == 0:
                    sp.dma_start(col[:, :, :], cols_n).then_inc(s_const, 16)
                    sp.dma_start(bias_up[:, :], cols_b).then_inc(s_const, 16)
                    load_weights(0)
                    load_weights(1)
            for dst, src in zip((gain2[:, :], shift2[:, :], bias_down[:, :], gain3[:, :], shift3[:, :]), rows_in):
                sp.dma_start(dst, src.partition_broadcast(P)).then_inc(s_const, 16)

            def body(g, par, first, last):
                for step in ffn_steps(first, last, first):
                    if step[0] == "prep":
                        load_weights(step[1])
                    elif step[0] == "load_n2":
                        b = step[1]
                        if first:
                            sp.wait_ge(s_wlo, 2 * FT)
                        else:
                            wait_alone(sp, s_store[b], g * 16)
                        load_n2(g + 1, 1 - par, b)
                    elif step[0] == "load_x":
                        wait_alone(sp, s_out, g * GB + (step[1] + 1 - GB))
                        load_x(g, step[1])
                    elif step[0] == "gain":
                        store(g - 1, 1 - par, step[1])
            run_pairs(sp, body)
            for b in range(GB):
                store(ngroups - 1, 1, b)
            for b in range(GB):
                sp.wait_ge(s_store[b], 16 * ngroups)

        @block.gpsimd
        def _(pool):
            nc.gpsimd.memset(ident[:, :], 0.0).then_inc(s_ident0, 1)
            nc.gpsimd.memset(neg_half[:, :], -0.5).then_inc(s_ident0, 1)
            pool.wait_ge(s_ident0, 2)
            nc.gpsimd.affine_select(out=ident[:, :], in_=ident[:, :], compare_op=ALU.not_equal, fill=1.0,
                                    base=0, pattern=[[-1, P]], channel_multiplier=1).then_inc(s_ident, 1)
            pool.wait_ge(s_const, 16 * 7)
            nc.gpsimd.tensor_tensor(shift2[:, :], shift2[:, :], bias_down[:, :], ALU.add).then_inc(s_shift2, 1)
            pool.wait_ge(s_shift2, 1)

            def residual(n, par, b):
                pool.wait_ge(s_turn, n + 1)
                nc.gpsimd.tensor_tensor(n_row[par][:, b, :], n_row[par][:, b, :], gain2[:, :], ALU.mult).then_inc(s_gain, 1)
                pool.wait_ge(s_gain, n + 1)
                nc.gpsimd.tensor_tensor(n_row[par][:, b, :], n_row[par][:, b, :], shift2[:, :], ALU.add).then_inc(s_res, 1)

            def finish(g, par, b):
                n = g * GB + b
                wait_alone(pool, s_mv, n + 1)
                nc.gpsimd.tensor_scalar(var[:, :], mv[:, b % 2, 1:2], LN_EPS, None, ALU.add).then_inc(s_var, 1)
                pool.wait_ge(s_var, n + 1)
                if not (isinstance(g, int) and n < 2):
                    pool.wait_ge(s_apply, n - 1)
                nc.gpsimd.tensor_tensor(ln[:, b % 2, 0:1], var[:, :], neg_half[:, :], ALU.pow).then_inc(s_rstd, 1)
                wait_alone(pool, s_rstd, n + 1)
                nc.gpsimd.tensor_scalar(ln[:, b % 2, 1:2], mv[:, b % 2, 0:1], ln[:, b % 2, 0:1], -1.0,
                                        ALU.mult, ALU.mult).then_inc(s_ln, 1)

            def shift_x(g, b):
                pool.wait_ge(s_xin[b], g * 16 + 16)
                nc.gpsimd.tensor_tensor(x_res[b][:, :], x_res[b][:, :], shift3[:, :], ALU.add).then_inc(s_xb, 1)

            def add_x(g, par, b):
                n = g * GB + b
                pool.wait_ge(s_gain3, n + 1)
                pool.wait_ge(s_xb, n + 1)
                nc.gpsimd.tensor_tensor(n_row[par][:, b, :], n_row[par][:, b, :], x_res[b][:, :], ALU.add).then_inc(s_out, 1)

            for b in range(GB):
                residual(b, 0, b)

            def body(g, par, first, last):
                for step in ffn_steps(first, last, first):
                    if step[0] == "turn":
                        residual(g * GB + (GB + step[1]), 1 - par, step[1])
                    elif step[0] == "finish":
                        finish(g - 1, 1 - par, step[1])
                    elif step[0] == "gain":
                        add_x(g - 1, 1 - par, step[1])
                    elif step[0] == "shift_x":
                        shift_x(g, step[1])
            run_pairs(pool, body)
            for b in range(GB):
                finish(ngroups - 1, 1, b)
                if b:
                    add_x(ngroups - 1, 1, b - 1)
            add_x(ngroups - 1, 1, GB - 1)

        @block.scalar
        def _(act):
            def turn_hi(n, par, b):
                act.wait_ge(s_turn, n + 1)
                nc.scalar.activation(nT_hi[par][:, :, b * P:(b + 1) * P], ps_turn[:, :].rearrange("p (k r) -> p k r", k=KT),
                                     ACT.Copy).then_inc(s_turn_hi, 1)

            def prep_hi(t):
                act.wait_ge(s_fold, t + 1)
                nc.scalar.activation(w1_hi[:, :, t * P:(t + 1) * P], stage1[t % 2], ACT.Copy).then_inc(s_whi, 1)
                act.wait_ge(s_w2in[t % 2], 16 * (t // 2 + 1))
                nc.scalar.activation(w2_hi[:, t, :], stage2[t % 2], ACT.Copy).then_inc(s_whi, 1)

            def apply(n, par, b):
                act.wait_ge(s_ln, n + 1)
                nc.scalar.activation(n_row[par][:, b, :], n_row[par][:, b, :], ACT.Identity, bias=ln[:, b % 2, 1:2],
                                     scale=ln[:, b % 2, 0:1]).then_inc(s_apply, 1)

            act.wait_ge(s_const, 16 * 7)
            for b in range(GB):
                turn_hi(b, 0, b)
                if b < 2:
                    prep_hi(b)

            def body(g, par, first, last):
                for step in ffn_steps(first, last, first):
                    if step[0] == "gelu":
                        t = step[1]
                        n = g * FT + t
                        act.wait_ge(s_up, n + 1)
                        if first and t < 2:
                            act.wait_ge(s_shift2, 1)
                        else:
                            act.wait_ge(s_act, n - 1)
                        if first:
                            act.wait_ge(s_bias, t + 1)
                        nc.scalar.activation(act_f[t % 2][:, :], ps_up[t % 2][:, :], ACT.Gelu,
                                             bias=bias_up[:, t:t + 1]).then_inc(s_gelu, 1)
                    elif step[0] == "prep":
                        prep_hi(step[1])
                    elif step[0] == "turn":
                        turn_hi(g * GB + (GB + step[1]), 1 - par, step[1])
                    elif step[0] == "finish":
                        apply(g * GB + (step[1] - GB), 1 - par, step[1])
            run_pairs(act, body)
            for b in range(GB):
                apply((ngroups - 1) * GB + b, 1, b)

        @block.vector
        def _(dve):
            def turn_lo(n, par, b):
                dve.wait_ge(s_turn_hi, n + 1)
                nc.vector.tensor_tensor(nT_lo[par][:, :, b * P:(b + 1) * P], ps_turn[:, :].rearrange("p (k r) -> p k r", k=KT),
                                        nT_hi[par][:, :, b * P:(b + 1) * P].bitcast(F32), ALU.subtract).then_inc(s_turn_lo, 1)

            def prep(t):
                dve.wait_ge(s_matvec, t + 1)
                nc.vector.tensor_tensor(bias_up[:, t:t + 1], ps_vec[:, t:t + 1], bias_up[:, t:t + 1], ALU.add).then_inc(s_bias, 1)
                nc.vector.tensor_tensor(stage1[t % 2], stage1[t % 2], col[:, 0, :].unsqueeze(2).broadcast_to([P, KT, P]),
                                        ALU.mult).then_inc(s_fold, 1)
                dve.wait_ge(s_whi, 2 * t + 1)
                nc.vector.tensor_tensor(w1_lo[:, :, t * P:(t + 1) * P], stage1[t % 2],
                                        w1_hi[:, :, t * P:(t + 1) * P].bitcast(F32), ALU.subtract).then_inc(s_wlo, 1)
                dve.wait_ge(s_whi, 2 * t + 2)
                nc.vector.tensor_tensor(w2_lo[:, t, :], stage2[t % 2], w2_hi[:, t, :].bitcast(F32),
                                        ALU.subtract).then_inc(s_wlo, 1)

            def stats(g, n, par, b):
                if not (isinstance(n, int) and n < 2):
                    dve.wait_ge(s_ln, n - 1)
                dve.wait_ge(s_sum, n + 1)
                nc.vector.bn_stats(st[:, b % 2, :], n_row[par][:, b, :]).then_inc(s_bn, 1)
                wait_alone(dve, s_bn, n + 1)
                nc.vector.bn_aggr(mv[:, b % 2, :], st[:, b % 2, :]).then_inc(s_mv, 1)

            def add_residual(g, par, b):
                n = g * GB + b
                dve.wait_ge(s_down, g * (FT * GB) + ((FT - 1) * GB + b + 1))
                dve.wait_ge(s_res, n + 1)
                nc.vector.tensor_tensor(n_row[par][:, b, :], ps_down[b][:, :], n_row[par][:, b, :], ALU.add).then_inc(s_sum, 1)

            def gain(n, par, b):
                dve.wait_ge(s_apply, n + 1)
                nc.vector.tensor_tensor(n_row[par][:, b, :], n_row[par][:, b, :], gain3[:, :], ALU.mult).then_inc(s_gain3, 1)

            dve.wait_ge(s_const, 16 * 7)
            for b in range(GB):
                turn_lo(b, 0, b)
                if b < 2:
                    prep(b)

            def body(g, par, first, last):
                for step in ffn_steps(first, last, first):
                    if step[0] == "split":
                        t = step[1]
                        n = g * FT + t
                        dve.wait_ge(s_gelu, n + 1)
                        if not (first and t < 2):
                            dve.wait_ge(s_down, g * (FT * GB) + (t - 1) * GB)
                        nc.vector.tensor_copy(act_hi[t % 2][:, :], act_f[t % 2][:, :]).then_inc(s_act_hi, 1)
                        dve.wait_ge(s_act_hi, n + 1)
                        nc.vector.tensor_tensor(act_lo[t % 2][:, :], act_f[t % 2][:, :], act_hi[t % 2][:, :].bitcast(F32),
                                                ALU.subtract).then_inc(s_act, 1)
                    elif step[0] == "prep":
                        prep(step[1])
                    elif step[0] == "add_res":
                        add_residual(g - 1, 1 - par, step[1])
                    elif step[0] == "finish":
                        stats(g - 1, g * GB + (step[1] - GB), 1 - par, step[1])
                    elif step[0] == "gain":
                        gain(g * GB + (step[1] - GB), 1 - par, step[1])
                    elif step[0] == "turn":
                        turn_lo(g * GB + (GB + step[1]), 1 - par, step[1])
            run_pairs(dve, body)
            for b in range(GB):
                add_residual(ngroups - 1, 1, b)
                stats(ngroups - 1, (ngroups - 1) * GB + b, 1, b)
                if b:
                    gain((ngroups - 1) * GB + b - 1, 1, b - 1)
            gain(ngroups * GB - 1, 1, GB - 1)

        @block.tensor
        def _(pe):
            def turn(n, g, par, b):
                pe.wait_ge(s_n2in[b], g * 16 + 16)
                wait(pe, s_turn_lo, n)
                for k in range(KT):
                    last = nc.tensor.transpose(ps_turn[:, k * P:(k + 1) * P], n_row[par][:, b, k * P:(k + 1) * P], ident[:, :])
                last.then_inc(s_turn, 1)

            def prep(t):
                pe.wait_ge(s_w1in[t % 2], 16 * (t // 2 + 1))
                wait(pe, s_bias, t)
                for k in range(KT):
                    last = nc.tensor.matmul(ps_vec[:, t:t + 1], stage1[t % 2][:, k, :], col[:, 1, k:k + 1],
                                            start=(k == 0), stop=(k == KT - 1))
                last.then_inc(s_matvec, 1)

            def down(g, t, first_group):
                pe.wait_ge(s_act, g * FT + (t + 1))
                if first_group:
                    pe.wait_ge(s_wlo, 2 * (t + 1))
                for b in range(GB):
                    if t == 0 and not first_group:
                        pe.wait_ge(s_sum, g * GB + (b + 1 - GB))
                    sl = slice(b * P, (b + 1) * P)
                    for i, (a, c) in enumerate(((act_hi, w2_hi), (act_hi, w2_lo), (act_lo, w2_hi))):
                        mm = nc.tensor.matmul(ps_down[b][:, :], a[t % 2][:, sl], c[:, t, :], start=(t == 0 and i == 0),
                                              stop=(t == FT - 1 and i == 2))
                    mm.then_inc(s_down, 1)

            pe.wait_ge(s_ident, 1)
            pe.wait_ge(s_const, 16 * 7)
            for b in range(GB):
                turn(b, 0, 0, b)
                if b < 2:
                    prep(b)

            def body(g, par, first, last):
                for step in ffn_steps(first, last, first):
                    if step[0] == "up":
                        t = step[1]
                        n = g * FT + t
                        if not (first and t < 2):
                            pe.wait_ge(s_gelu, n - 1)
                        if t == 0:
                            pe.wait_ge(s_turn_lo, g * GB + GB)
                        if first:
                            pe.wait_ge(s_wlo, 2 * t + 1)
                        for k in range(KT):
                            for i, (a, c) in enumerate(((w1_hi, nT_hi), (w1_hi, nT_lo), (w1_lo, nT_hi))):
                                mm = nc.tensor.matmul(ps_up[t % 2][:, :], a[:, k, t * P:(t + 1) * P], c[par][:, k, :],
                                                      start=(k == 0 and i == 0), stop=(k == KT - 1 and i == 2))
                        mm.then_inc(s_up, 1)
                    elif step[0] == "prep":
                        prep(step[1])
                    elif step[0] == "down":
                        if step[1] < 0:
                            down(g - 1, FT - 1, False)
                        else:
                            down(g, step[1], first)
                    elif step[0] == "turn":
                        turn(g * GB + (GB + step[1]), g + 1, 1 - par, step[1])
            run_pairs(pe, body)
            down(ngroups - 1, FT - 1, False)


def kernel(**inputs):
    import numpy as np
    import concourse.bacc as _bacc
    from concourse import mybir as _mybir
    from concourse.bass_utils import run_bass_kernel_spmd as _run

    pre = "L0_gnn_"

    def col(name):
        return np.asarray(inputs[pre + name]).reshape(-1, P).T

    arrays = {"x": np.ascontiguousarray(inputs["x"]), "adj": np.ascontiguousarray(inputs["adj"])}
    weights = (("q", "n2e_q"), ("k", "n2e_k"), ("v", "n2e_v"), ("q2", "e2n_q"), ("ek", "e2n_k"), ("ev", "e2n_v"))
    for short, name in weights:
        arrays[f"w_{short}"] = np.ascontiguousarray(np.asarray(inputs[f"{pre}{name}_w"]).T)
    for short in ("ffn_w1", "ffn_w2"):
        arrays[short] = np.ascontiguousarray(np.asarray(inputs[pre + short]).T)
    arrays["cols"] = np.ascontiguousarray(np.stack([col(n) for n in (
        "n2e_q_b", "n2e_k_b", "e2n_q_b", "e2n_k_b", "norm1_g", "norm1_b")], axis=1))
    arrays["cols_norm2"] = np.ascontiguousarray(np.stack([col("norm2_g"), col("norm2_b")], axis=1))
    arrays["cols_ffn_b1"] = np.ascontiguousarray(col("ffn_b1"))
    rows = ("n2e_v_b", "e2n_v_b", "norm2_g", "norm2_b", "ffn_b2", "norm3_g", "norm3_b")
    for name in rows:
        arrays[name] = np.ascontiguousarray(inputs[pre + name])
    nc = _bacc.Bacc("TRN2", target_bir_lowering=False, num_devices=1)
    ap = {n: nc.dram_tensor(f"in_{n}", a.shape, _mybir.dt.from_np(a.dtype), kind="ExternalInput").ap()
          for n, a in arrays.items()}
    shape = tuple(inputs["x"].shape)
    n2 = nc.dram_tensor("n2_scratch", shape, _mybir.dt.float32, kind="Internal").ap()
    out = nc.dram_tensor("out_0", shape, _mybir.dt.float32, kind="ExternalOutput").ap()
    attention_pass(nc, ap["x"], ap["adj"], {k: ap[f"w_{k}"] for k, _ in weights}, ap["cols"],
                   tuple(ap[n] for n in rows[:2]), n2)
    ffn_pass(nc, n2, ap["x"], ap["ffn_w1"], ap["ffn_w2"], (ap["cols_norm2"], ap["cols_ffn_b1"]),
             tuple(ap[n] for n in rows[2:]), out)
    r = _run(nc, [{f"in_{n}": a for n, a in arrays.items()}], core_ids=[0])
    return r.results[0]["out_0"]
```

```python
from contextlib import ExitStack

import concourse.bass as bass
from concourse import mybir

F32 = mybir.dt.float32
F32R = mybir.dt.float32r
BF16 = mybir.dt.bfloat16
ALU = mybir.AluOpType
ACT = mybir.ActivationFunctionType
AX = mybir.AxisListType

P = 128
D = 512
KT = D // P
H = 8
HD = D // H
HU = H // 2
HV = HD + 1
GB = 4
R = GB * P
DF = 2048
FT = DF // P
LN_EPS = 1e-5
SCALE = HD ** -0.5
MASKED = -1e30

UNITS = 4 * GB
TILES = 24
PRO_TILES = 12
TILE_KIND = ([("q2", 0), ("q2", 1), ("q2", 2), ("ev", 0), ("q2", 3), ("ev", 1), ("ev", 2)]
             + [("ek", m) for m in range(KT)] + [("ev", 3)]
             + [(w, m) for m in range(KT) for w in ("q", "k")] + [("v", b) for b in range(GB)])
TILE_OF = {k: t for t, k in enumerate(TILE_KIND)}
HALVES_L0 = (1,) * 8
HALVES_L1 = (3,) * 8
NEXT_AT = (2, 3, 4, 5)
TRANSPOSES = 8


class Early:

    def __init__(self, nc, ctx):
        def sb(name, shape, dt=F32):
            return ctx.enter_context(nc.sbuf_tensor(name, shape, dt))

        self.ident, self.neg_half = sb("ident", [P, P]), sb("neg_half", [P, 1])
        self.rows, self.stage = sb("early_rows", [P, GB, D]), sb("early_stage", [P, GB, D])
        self.nT_hi, self.nT_lo = sb("early_nT_hi", [P, KT, R], F32R), sb("early_nT_lo", [P, KT, R], F32R)
        self.col, self.bias_up = sb("early_col", [P, 2, KT]), sb("early_bias_up", [P, FT])
        self.stage1 = [self.stage[:, 2 * i, :].rearrange("p (k n) -> p k n", k=KT) for i in range(2)]
        self.stage2 = [self.stage[:, 2 * i + 1, :] for i in range(2)]
        self.s_ident = ctx.enter_context(nc.semaphore("s_ident"))


def w1_tiles(w1):
    return w1.rearrange("(k p) (t n) -> t p k n", p=P, n=P)


def w2_tiles(w2):
    return w2.rearrange("(t p) n -> t p n", p=P)


def steps_of_group(first, last):
    out = []

    def halves(lo, hi):
        for n in range(lo, hi):
            out.append(("half", n // 2, n % 2))
            if n % 2 == 1:
                out.append(("evac", n // 2))

    def tile(kind, idx):
        t = TILE_OF[(kind, idx)]
        halves(2 * t, 2 * t + 2)

    def finish(u):
        out.extend([("pt", u), ("pt_evac", u)])

    def values(u):
        out.extend([("av", u), ("norm", u), ("add_h", u)])

    for u in range(UNITS):
        layer, v = divmod(u, 8)
        out.extend([("scores", u), ("shift", u)])
        prev = u - 1 if u else -1
        has_prev = u not in (0, 8) or (u == 0 and not first)
        if v % 2 == 0:
            b = v // 2 - 2
            if b >= 0:
                out.append(("apply", layer, b))
            elif layer == 0 and not first:
                out.append(("apply", -1, b + 4))
        if has_prev:
            finish(prev)
        out.append(("exp", u))
        if v % 2 == 0:
            out.append(("h_again", layer, v // 2))
        if not last and u in (5, 7):
            out.append(("relu_x", (u - 5) // 2))
        if v in (3, 5, 7):
            out.append(("ln_row", layer, (v - 3) // 2))
        if u == 1 and not first:
            out.append(("ln_row", -1, 3))
        if u == 0 and not first:
            out.append(("mask", 0, 3))
        if u == 1 and not last:
            out.append(("load_adj",))
        if not last and u in (4, 6):
            out.append(("ln_x", (u - 4) // 2))
        if layer == 0:
            halves(sum(HALVES_L0[:v]), sum(HALVES_L0[:v + 1]))
        elif not last:
            halves(24 + sum(HALVES_L1[:v]), 24 + sum(HALVES_L1[:v + 1]))
        elif v in NEXT_AT:
            out.extend([("t_next", NEXT_AT.index(v)), ("t_evac", "next", NEXT_AT.index(v))])
        if last and u == 7:
            out.append(("load_early",))
        if has_prev:
            values(prev)
        if u == 0:
            out.append(("load_h", 0, 1))
            if not last:
                out.extend([("load_x", 0), ("load_x", 1)])
        if v >= 2 and v % 2 == 0:
            nb = v // 2 + 1
            if nb < GB:
                out.append(("load_h", layer, nb))
            elif layer == 0:
                out.append(("load_h", 1, 0))
            elif not last:
                out.append(("load_h", 2, 0))
        if not last and layer == 1 and v in (2, 4, 6):
            out.append(("mask", 1, v // 2 - 1))
        if not last and u == 15:
            out.append(("keep_stats",))
        if layer == 0 and v in (4, 6):
            out.extend([("t_edge", v // 2 - 2), ("t_evac", "edge", v // 2 - 2)])
        if u == 7:
            finish(7)
            out.append(("apply", 0, 2))
            halves(8, 9)
            values(7)
            halves(9, 10)
            out.append(("load_h", 1, 1))
            out.extend([("t_edge", 2), ("t_evac", "edge", 2), ("ln_row", 0, 3)])
            tile("ev", 1)
            if not last:
                out.extend([("t_h", 0), ("t_evac", "h", 0), ("load_x", 2)])
            out.append(("apply", 0, 3))
            halves(12, 13)
            out.extend([("t_edge", 3), ("t_evac", "edge", 3)])
            halves(13, 14)
            tile("ek", 0)
            if not last:
                out.extend([("t_h", 1), ("t_evac", "h", 1), ("load_x", 3), ("ln_x", 2), ("relu_x", 2)])
            tile("ek", 1)
            if not last:
                out.extend([("ln_x", 3), ("relu_x", 3)])
            tile("ek", 2)
            if not last:
                out.extend([("t_h", 2), ("t_evac", "h", 2)])
            tile("ek", 3)
            if not last:
                out.extend([("t_h", 3), ("t_evac", "h", 3)])
            tile("ev", 3)
    return out


def wait(eng, sem, value):
    if isinstance(value, int) and value <= 0:
        return
    eng.wait_ge(sem, value)


def wait_alone(eng, sem, value):
    if isinstance(value, int) and value <= 0:
        return
    eng.wait_ge(sem, value)
    eng.nop(nofuse=True)


def attention_pass(nc, early, x, adj, w, cols, rows_in, n2, w1, w2, cols_ffn):
    ident, neg_half, s_ident = early.ident, early.neg_half, early.s_ident
    ngroups = x.shape[0] // GB
    W_ORDER = ["q", "k", "v", "q2", "ek", "ev"]
    COL = {"q": 0, "k": 1, "q2": 2, "ek": 3, "g1": 4, "b1": 5}
    x_v = x.rearrange("(g b) p d -> g b p d", b=GB)
    n2_v = n2.rearrange("(g b) p d -> g b p d", b=GB)
    adj_v = adj.rearrange("(g b) i j -> g i b j", b=GB)

    def graph(view, g, b):
        if isinstance(g, int):
            return view[g, b]
        return view[bass.ds(g, 1), b].rearrange("o p d -> (o p) d")

    ctx = ExitStack()
    with ctx:
        def sb(name, shape, dt=F32):
            return ctx.enter_context(nc.sbuf_tensor(name, shape, dt))

        def sem(name):
            return ctx.enter_context(nc.semaphore(name))

        w_hi = {"q": early.nT_hi}
        w_lo = {"q": early.nT_lo}
        for k in W_ORDER:
            for part, name in ((w_hi, "hi"), (w_lo, "lo")):
                if k not in part:
                    part[k] = sb(f"w_{k}_{name}", [P, KT, D], F32R)
        hT_hi, hT_lo = sb("hT_hi", [P, KT, R], F32R), sb("hT_lo", [P, KT, R], F32R)
        eT_hi, eT_lo = sb("eT_hi", [P, KT, R], F32R), sb("eT_lo", [P, KT, R], F32R)
        proj = {"q": early.rows, "k": early.stage, "q2": sb("proj_q2", [P, KT, R]), "ek": sb("proj_ek", [P, KT, R])}
        val = {k: sb(f"val_{k}", [P, GB, H, HV]) for k in ("v", "ev")}
        h_row = [sb(f"h_row{i}", [P, D]) for i in range(2)]
        x_row = [sb(f"x_row{i}", [P, D]) for i in range(2)]
        row = [sb(f"row{i}", [P, D]) for i in range(GB)]
        prob = [sb(f"prob{i}", [P, HU * P]) for i in range(2)]
        probT = sb("probT", [P, HU * P])
        bias_row = {"v": sb("bias_v", [P, D]), "ev": sb("bias_ev", [P, D])}
        col = sb("col", [P, 6, KT])
        adj_in = sb("adj_in", [P, GB, P])
        mask = sb("mask", [P, GB, P], BF16)
        ident_b = sb("ident_b", [P, P], BF16)
        peak = sb("peak", [P, 2, HU])
        recip = sb("recip", [P, 2, HU])
        st_row, st_x = sb("st_row", [P, GB, 6]), sb("st_x", [P, 2, 6])
        mv_row, mv_x = sb("mv_row", [P, GB, 2]), sb("mv_x", [P, 2, 2])
        var_row, var_x = sb("var_row", [P, 1]), sb("var_x", [P, 1])
        ln_row = sb("ln_row", [P, GB, 2])
        ln_next, ln_cur = sb("ln_next", [P, GB, 2]), sb("ln_cur", [P, GB, 2])

        bank = [ctx.enter_context(nc.psum_tensor(f"bank{i}", [P, 512], F32)) for i in range(8)]
        ps_scores, ps_tile, ps_av = bank[0:2], bank[2:4], bank[4:6]
        ps_probT, ps_turn = bank[6], bank[7]

        s_const = sem("s_const")
        s_ident0 = sem("s_ident0")
        s_ones = sem("s_ones")
        s_stage = [sem(f"s_stage{i}") for i in range(2)]
        s_matvec = sem("s_matvec")
        s_bias = sem("s_bias")
        s_fold = sem("s_fold")
        s_whi, s_wlo = sem("s_whi"), sem("s_wlo")
        s_adj = sem("s_adj")
        s_mask = sem("s_mask")
        s_masked = sem("s_masked")
        s_xin = [sem(f"s_xin{i}") for i in range(2)]
        s_xfirst = [sem(f"s_xfirst{i}") for i in range(2)]
        s_hin = [sem(f"s_hin{i}") for i in range(2)]
        s_hagain = sem("s_hagain")
        s_scores, s_peak, s_shift, s_exp = sem("s_scores"), sem("s_peak"), sem("s_shift"), sem("s_exp")
        s_pt, s_pt_evac = sem("s_pt"), sem("s_pt_evac")
        s_av, s_recip, s_norm, s_add = sem("s_av"), sem("s_recip"), sem("s_norm"), sem("s_add")
        s_tile = sem("s_tile")
        s_evac = [sem(f"s_evac{i}") for i in range(2)]
        s_turn, s_turn_hi, s_turn_lo = sem("s_turn"), sem("s_turn_hi"), sem("s_turn_lo")
        s_bn_row, s_mv_row, s_var_row, s_rstd_row, s_ln_row = (sem(f"s_{n}_row") for n in ("bn", "mv", "var", "rstd", "ln"))
        s_bn_x, s_mv_x, s_var_x, s_rstd_x, s_ln_x = (sem(f"s_{n}_x") for n in ("bn", "mv", "var", "rstd", "ln"))
        s_apply, s_relu, s_keep = sem("s_apply"), sem("s_relu"), sem("s_keep")
        s_store = [sem(f"s_store{i}") for i in range(GB)]
        s_early_rows = [sem(f"s_early_rows{i}") for i in range(GB)]
        s_early_w, s_early_col = sem("s_early_w"), sem("s_early_col")
        s_next = sem("s_next")

        def turn_no(g, kind, b):
            order = {"edge": (0, 1, 2, 4), "h": (3, 5, 6, 7), "next": ()}[kind]
            if isinstance(g, int) and g == ngroups - 1:
                order = {"edge": range(GB), "next": range(GB, 2 * GB)}[kind]
            return GB + TRANSPOSES * g + order[b]

        def wait_tile(eng, g, t):
            wait(eng, s_evac[t % 2], (PRO_TILES + TILES * g) // 2 + t // 2 + 1 if isinstance(g, int)
                 else g * (TILES // 2) + (PRO_TILES // 2 + t // 2 + 1))

        def parity_heads(ap, par):
            return ap.rearrange("p (j two d) -> p two j d", two=2, d=HD)[:, par]

        def run_groups(eng, body):
            body(0, True, False)
            with eng.Fori(1, ngroups - 1) as g:
                body(g, False, False)
            body(ngroups - 1, False, True)

        block = ctx.enter_context(nc.Block())

        @block.sync
        def _(sp):
            def load_x(g, b):
                sp.dma_start(x_row[b % 2][:, :], graph(x_v, g, b)).then_inc(s_xin[b % 2], 16)

            def load_h(g, b):
                sp.dma_start(h_row[b % 2][:, :], graph(x_v, g, b)).then_inc(s_hin[b % 2], 16)

            def load_adj(g):
                src = adj_v[g] if isinstance(g, int) else adj_v[bass.ds(g, 1)].rearrange("o i b j -> (o i) b j")
                sp.dma_start(adj_in[:, :, :], src).then_inc(s_adj, 16)

            def store_n2(g, b):
                wait_alone(sp, s_store[(b - 1) % GB], (g + (1 if b else 0)) * 16)
                sp.dma_start(graph(n2_v, g, b), row[b][:, :]).then_inc(s_store[b], 16)

            load_x(0, 0)
            load_x(0, 1)
            for b in (2, 3):
                sp.dma_start(h_row[b % 2][:, :], graph(x_v, 0, b)).then_inc(s_xfirst[b % 2], 16)
            stage = (proj["q2"], proj["ek"])
            for i, k in enumerate(W_ORDER):
                if i >= 2:
                    sp.wait_ge(s_wlo, i - 1)
                sp.dma_start(stage[i % 2][:, :, :], w[k].rearrange("(k p) n -> p k n", p=P)).then_inc(s_stage[i % 2], 16)
                if i == 1:
                    sp.dma_start(col[:, :, :], cols).then_inc(s_const, 16)
                    for kk, src in zip(("v", "ev"), rows_in):
                        sp.dma_start(bias_row[kk][:, :], src.partition_broadcast(P)).then_inc(s_const, 16)
                    load_adj(0)
            sp.wait_ge(s_turn, 4)
            load_h(0, 0)

            def body(g, first, last):
                for step in steps_of_group(first, last):
                    if step[0] == "load_x":
                        b = step[1]
                        if b < 2:
                            wait_alone(sp, s_turn, 4 if first else turn_no(g - 1, "h", b + 2) + 1)
                        else:
                            wait_alone(sp, s_turn, turn_no(g, "h", b - 2) + 1)
                        load_x(g + 1, b)
                    elif step[0] == "load_h":
                        layer, b = step[1:]
                        unit = 8 * layer + 2 * b - 3
                        wait_alone(sp, s_add, g * UNITS + unit + 1 if not (first and unit < 0) else 0)
                        load_h(g + 1 if layer == 2 else g, b)
                    elif step[0] == "load_adj":
                        wait_alone(sp, s_mask, g * GB + GB)
                        load_adj(g + 1)
                    elif step[0] == "apply" and step[1] != 0:
                        gg, b = (g if step[1] == 1 else g - 1), step[2]
                        wait_alone(sp, s_apply, gg * 8 + 4 + b + 1)
                        store_n2(gg, b)
                    elif step[0] == "load_early":
                        sp.wait_ge(s_scores, g * UNITS + 8)
                        for dst, src in ((early.col[:, :, :], cols_ffn[0]), (early.bias_up[:, :], cols_ffn[1])):
                            sp.dma_start(dst, src).then_inc(s_early_col, 16)
                        for b in range(GB):
                            sp.dma_start(early.rows[:, b, :], n2_v[0, b]).then_inc(s_early_rows[b], 16)
                        for t in range(2):
                            sp.dma_start(early.stage1[t], w1_tiles(w1)[t]).then_inc(s_early_w, 16)
                            sp.dma_start(early.stage2[t], w2_tiles(w2)[t]).then_inc(s_early_w, 16)
            run_groups(sp, body)
            for b in (2, 3):
                sp.wait_ge(s_apply, 8 * (ngroups - 1) + 4 + b + 1)
                store_n2(ngroups - 1, b)
            for b in range(GB):
                sp.wait_ge(s_store[b], 16 * ngroups)
            sp.wait_ge(s_early_w, 16 * 4)

        @block.gpsimd
        def _(pool):
            nc.gpsimd.memset(ident[:, :], 0.0).then_inc(s_ident0, 1)
            nc.gpsimd.memset(ident_b[:, :], 0.0).then_inc(s_ident0, 1)
            nc.gpsimd.memset(neg_half[:, :], -0.5).then_inc(s_ident0, 1)
            pool.wait_ge(s_ident0, 3)
            for m in (ident, ident_b):
                nc.gpsimd.affine_select(out=m[:, :], in_=m[:, :], compare_op=ALU.not_equal, fill=1.0,
                                        base=0, pattern=[[-1, P]], channel_multiplier=1).then_inc(s_ident, 1)

            def make_mask(g, b):
                wait_alone(pool, s_adj, g * 16 + 16)
                nc.gpsimd.tensor_scalar(mask[:, b, :], adj_in[:, b, :], 0.0, MASKED, ALU.is_le, ALU.mult).then_inc(s_mask, 1)

            def norm_factors(n, mv, var, rstd, shift, s_mv, s_var, s_rstd, s_ln):
                wait_alone(pool, s_mv, n + 1)
                nc.gpsimd.tensor_scalar(var[:, :], mv[:, 1:2], LN_EPS, None, ALU.add).then_inc(s_var, 1)
                pool.wait_ge(s_var, n + 1)
                nc.gpsimd.tensor_tensor(rstd, var[:, :], neg_half[:, :], ALU.pow).then_inc(s_rstd, 1)
                wait_alone(pool, s_rstd, n + 1)
                nc.gpsimd.tensor_scalar(shift, mv[:, 0:1], rstd, -1.0, ALU.mult, ALU.mult).then_inc(s_ln, 1)

            def ln_x(n, b):
                norm_factors(n, mv_x[:, b % 2, :], var_x, ln_next[:, b, 0:1], ln_next[:, b, 1:2],
                             s_mv_x, s_var_x, s_rstd_x, s_ln_x)

            def ln_rows(n, b):
                if not (isinstance(n, int) and n < 2):
                    wait_alone(pool, s_apply, n - 1)
                norm_factors(n, mv_row[:, b, :], var_row, ln_row[:, b, 0:1], ln_row[:, b, 1:2],
                             s_mv_row, s_var_row, s_rstd_row, s_ln_row)

            for b in range(GB):
                ln_x(b, b)
            for b in range(GB):
                make_mask(0, b)

            def body(g, first, last):
                for step in steps_of_group(first, last):
                    if step[0] == "mask":
                        b = step[2]
                        gg = g + step[1]
                        wait_alone(pool, s_masked, (gg - 1) * 8 + 2 * b + 2)
                        make_mask(gg, b)
                    elif step[0] == "ln_x":
                        b = step[1]
                        wait_alone(pool, s_keep, g + 1)
                        ln_x(g * GB + (GB + b), b)
                    elif step[0] == "ln_row":
                        ln_rows(g * 8 + 4 * step[1] + step[2], step[2])
                    elif step[0] == "add_h":
                        u = step[1]
                        b, par = (u % 8) // 2, u % 2
                        n = g * UNITS + u
                        pool.wait_ge(s_norm, n + 1)
                        pool.wait_ge(s_hagain, g * 8 + u // 2 + 1)
                        out = parity_heads(row[b][:, :], par)
                        nc.gpsimd.tensor_tensor(out, out, parity_heads(h_row[b % 2][:, :], par), ALU.add).then_inc(s_add, 1)
            run_groups(pool, body)
            n = ngroups * UNITS - 1
            pool.wait_ge(s_norm, n + 1)
            out = parity_heads(row[3][:, :], 1)
            nc.gpsimd.tensor_tensor(out, out, parity_heads(h_row[1][:, :], 1), ALU.add).then_inc(s_add, 1)
            ln_rows(ngroups * 8 - 1, 3)

        @block.scalar
        def _(act):
            def relu_x(n, b, rows=x_row):
                act.wait_ge(s_ln_x, n + 1)
                nc.scalar.activation(rows[b % 2][:, :], rows[b % 2][:, :], ACT.Relu, bias=ln_next[:, b, 1:2],
                                     scale=ln_next[:, b, 0:1]).then_inc(s_relu, 1)

            def turn_hi(no, kind, b):
                wait(act, s_turn, no + 1)
                if kind == "next":
                    if b == 0:
                        act.wait_ge(s_early_col, 32)
                    else:
                        act.wait_ge(s_turn_lo, no)
                    for k in range(KT):
                        last_k = nc.scalar.activation(x_row[0][:, k * P:(k + 1) * P], ps_turn[:, k * P:(k + 1) * P],
                                                      ACT.Identity, bias=early.col[:, 1, k:k + 1], scale=early.col[:, 0, k:k + 1])
                    last_k.then_inc(s_next, 1)
                    return
                dst = hT_hi if kind == "h" else eT_hi
                nc.scalar.activation(dst[:, :, b * P:(b + 1) * P], ps_turn[:, :].rearrange("p (k r) -> p k r", k=KT),
                                     ACT.Copy).then_inc(s_turn_hi, 1)

            def split_hi(i):
                if i < 4:
                    act.wait_ge(s_stage[i % 2], 16 * (i // 2 + 1))
                else:
                    act.wait_ge(s_fold, i - 3)
                nc.scalar.activation(w_hi[W_ORDER[i]][:, :, :], (proj["q2"], proj["ek"])[i % 2][:, :, :],
                                     ACT.Copy).then_inc(s_whi, 1)

            def evac(no, t):
                kind, m = TILE_KIND[t]
                if kind in ("v", "ev"):
                    return
                wait(act, s_tile, no + 1)
                nc.scalar.activation(proj[kind][:, m, :], ps_tile[t % 2][:, :], ACT.Identity,
                                     bias=col[:, COL[kind], m:m + 1]).then_inc(s_evac[t % 2], 1)

            def keep():
                nc.scalar.activation(ln_cur[:, :, :], ln_next[:, :, :], ACT.Copy).then_inc(s_keep, 1)

            def apply(n, b):
                act.wait_ge(s_ln_row, n + 1)
                nc.scalar.activation(row[b][:, :], row[b][:, :], ACT.Identity, bias=ln_row[:, b, 1:2],
                                     scale=ln_row[:, b, 0:1]).then_inc(s_apply, 1)

            for b in range(GB):
                relu_x(b, b, x_row if b < 2 else h_row)
                if b:
                    turn_hi(b - 1, "h", b - 1)
            turn_hi(GB - 1, "h", GB - 1)
            split_hi(0)
            split_hi(1)
            keep()
            act.wait_ge(s_const, 48)
            for t in range(TILES - PRO_TILES, TILES):
                evac(t - PRO_TILES, t)
                if t - (TILES - PRO_TILES) in (1, 3):
                    split_hi((t - (TILES - PRO_TILES)) // 2 + 2)
            split_hi(4)
            split_hi(5)

            def pt_evac(n, u):
                act.wait_ge(s_pt, n + 1)
                nc.scalar.activation(probT[:, :], ps_probT[:, :], ACT.Copy).then_inc(s_pt_evac, 1)

            def body(g, first, last):
                for step in steps_of_group(first, last):
                    if step[0] == "pt_evac":
                        pt_evac(g * UNITS + step[1], step[1] % UNITS)
                    elif step[0] == "h_again":
                        layer, b = step[1:]
                        act.wait_ge(s_hin[b % 2], g * 64 + 16 * (2 * layer + b // 2 + 1))
                        act.wait_ge(s_keep, g + 1)
                        nc.scalar.activation(h_row[b % 2][:, :], h_row[b % 2][:, :], ACT.Relu, bias=ln_cur[:, b, 1:2],
                                             scale=ln_cur[:, b, 0:1]).then_inc(s_hagain, 1)
                    elif step[0] == "exp":
                        u = step[1]
                        act.wait_ge(s_shift, g * UNITS + u + 1)
                        nc.scalar.activation(prob[u % 2][:, :], prob[u % 2][:, :], ACT.Exp, scale=SCALE).then_inc(s_exp, 1)
                    elif step[0] == "evac":
                        evac(g * TILES + (PRO_TILES + step[1]), step[1])
                    elif step[0] == "apply":
                        apply(g * 8 + 4 * step[1] + step[2], step[2])
                    elif step[0] == "relu_x":
                        relu_x(g * GB + (GB + step[1]), step[1])
                    elif step[0] == "t_evac":
                        turn_hi(turn_no(g, step[1], step[2]), step[1], step[2])
                    elif step[0] == "keep_stats":
                        act.wait_ge(s_hagain, g * 8 + 8)
                        keep()
            run_groups(act, body)
            apply(ngroups * 8 - 2, 2)
            pt_evac(ngroups * UNITS - 1, UNITS - 1)
            apply(ngroups * 8 - 1, 3)

        @block.vector
        def _(dve):
            for k in ("v", "ev"):
                last_ones = nc.vector.memset(val[k][:, :, :, HD:HV], 1.0).then_inc(s_ones, 1)

            def stats(n, src, st, mv, s_bn, s_mv):
                nc.vector.bn_stats(st, src).then_inc(s_bn, 1)
                wait_alone(dve, s_bn, n + 1)
                nc.vector.bn_aggr(mv, st).then_inc(s_mv, 1)

            def ln_x(g, n, b, rows=x_row):
                if rows is h_row:
                    dve.wait_ge(s_xfirst[b % 2], 16)
                else:
                    dve.wait_ge(s_xin[b % 2], g * 32 + 16 * (b // 2 + (1 if isinstance(g, int) and g == 0 else 0)))
                if not (isinstance(n, int) and n < 2):
                    dve.wait_ge(s_ln_x, n - 1)
                stats(n, rows[b % 2][:, :], st_x[:, b % 2, :], mv_x[:, b % 2, :], s_bn_x, s_mv_x)

            def ln_rows(n, b, unit_no):
                dve.wait_ge(s_add, unit_no + 1)
                stats(n, row[b][:, :], st_row[:, b, :], mv_row[:, b, :], s_bn_row, s_mv_row)

            def turn_lo(no, kind, b):
                if kind == "next":
                    src = x_row[0][:, :].rearrange("p (k r) -> p k r", k=KT)
                    hi = early.nT_hi[:, :, b * P:(b + 1) * P]
                    dve.wait_ge(s_next, b + 1)
                    nc.vector.tensor_copy(hi, src).then_inc(s_turn_hi, 1)
                    dve.wait_ge(s_turn_hi, no + 1)
                    nc.vector.tensor_tensor(early.nT_lo[:, :, b * P:(b + 1) * P], src, hi.bitcast(F32),
                                            ALU.subtract).then_inc(s_turn_lo, 1)
                    return
                hi, lo = (hT_hi, hT_lo) if kind == "h" else (eT_hi, eT_lo)
                dve.wait_ge(s_turn_hi, no + 1)
                nc.vector.tensor_tensor(lo[:, :, b * P:(b + 1) * P], ps_turn[:, :].rearrange("p (k r) -> p k r", k=KT),
                                        hi[:, :, b * P:(b + 1) * P].bitcast(F32), ALU.subtract).then_inc(s_turn_lo, 1)

            def split_lo(i):
                k = W_ORDER[i]
                stage = (proj["q2"], proj["ek"])[i % 2]
                if i >= 4:
                    dve.wait_ge(s_stage[i % 2], 16 * (i // 2 + 1))
                    dve.wait_ge(s_matvec, i - 3)
                    if k == "ek":
                        nc.vector.tensor_tensor(col[:, COL["ek"], :], ps_av[0][:, 0:KT], col[:, COL["ek"], :],
                                                ALU.add).then_inc(s_bias, 1)
                    else:
                        nc.vector.tensor_tensor(bias_row["ev"][:, :], ps_av[1][:, :], bias_row["ev"][:, :],
                                                ALU.add).then_inc(s_bias, 1)
                    for t in range(KT):
                        folded = nc.vector.tensor_scalar(stage[:, t, :], stage[:, t, :], col[:, COL["g1"], t:t + 1],
                                                         None, ALU.mult)
                    folded.then_inc(s_fold, 1)
                dve.wait_ge(s_whi, i + 1)
                nc.vector.tensor_tensor(w_lo[k][:, :, :], stage[:, :, :], w_hi[k][:, :, :].bitcast(F32),
                                        ALU.subtract).then_inc(s_wlo, 1)

            def evac(no, t):
                kind, b = TILE_KIND[t]
                if kind not in ("v", "ev"):
                    return
                wait(dve, s_tile, no + 1)
                nc.vector.tensor_tensor(val[kind][:, b, :, 0:HD], ps_tile[t % 2][:, :].rearrange("p (h d) -> p h d", h=H),
                                        bias_row[kind][:, :].rearrange("p (h d) -> p h d", h=H),
                                        ALU.add).then_inc(s_evac[t % 2], 1)

            for b in range(GB):
                ln_x(0, b, b, x_row if b < 2 else h_row)
            for b in range(GB):
                turn_lo(b, "h", b)
            for i in range(4):
                split_lo(i)
            dve.wait_ge(s_const, 48)
            split_lo(4)
            for b in range(GB):
                evac(8 + b, TILE_OF[("v", b)])
                if b == 1:
                    split_lo(5)
            dve.wait_ge(s_bias, 2)

            def normalise(g, n, u):
                layer, b, par = (u % UNITS) // 8, (u % 8) // 2, u % 2
                dve.wait_ge(s_av, n + 1)
                src = ps_av[par][:, 0:HU * HV].rearrange("p (j d) -> p j d", d=HV)
                nc.vector.reciprocal(recip[:, par, :], src[:, :, HD]).then_inc(s_recip, 1)
                if par == 0 and layer == 0:
                    wait(dve, s_store[b], g * 16)
                elif par == 0:
                    dve.wait_ge(s_turn, turn_no(g, "edge", b) + 1)
                dve.wait_ge(s_recip, n + 1)
                nc.vector.tensor_tensor(parity_heads(row[b][:, :], par), src[:, :, 0:HD],
                                        recip[:, par, :].unsqueeze(2).broadcast_to([P, HU, HD]), ALU.mult).then_inc(s_norm, 1)

            def body(g, first, last):
                for step in steps_of_group(first, last):
                    if step[0] == "shift":
                        u = step[1]
                        n = g * UNITS + u
                        src = ps_scores[u % 2][:, :].rearrange("p (j k) -> p j k", j=HU)
                        dve.wait_ge(s_scores, n + 1)
                        dst = prob[u % 2][:, :].rearrange("p (j k) -> p j k", j=HU)
                        if u >= 8:
                            dve.wait_ge(s_pt, n - 1)
                            nc.vector.tensor_tensor(dst, src, mask[:, (u - 8) // 2, :].unsqueeze(1).broadcast_to([P, HU, P]),
                                                    ALU.add).then_inc(s_masked, 1)
                            src = dst
                            dve.wait_ge(s_masked, g * 8 + (u - 7))
                        nc.vector.tensor_reduce(peak[:, u % 2, :], src, AX.X, ALU.max).then_inc(s_peak, 1)
                        if u < 8 and not (first and u < 2):
                            dve.wait_ge(s_pt, n - 1)
                        dve.wait_ge(s_peak, n + 1)
                        nc.vector.tensor_tensor(dst, src,
                                                peak[:, u % 2, :].unsqueeze(2).broadcast_to([P, HU, P]),
                                                ALU.subtract).then_inc(s_shift, 1)
                    elif step[0] == "norm":
                        normalise(g, g * UNITS + step[1], step[1])
                    elif step[0] == "evac":
                        evac(g * TILES + (PRO_TILES + step[1]), step[1])
                    elif step[0] == "ln_row":
                        layer, b = step[1:]
                        ln_rows(g * 8 + 4 * layer + b, b, g * UNITS + 8 * layer + 2 * b + 1)
                    elif step[0] == "ln_x":
                        ln_x(g + 1, g * GB + (GB + step[1]), step[1])
                    elif step[0] == "t_evac":
                        turn_lo(turn_no(g, step[1], step[2]), step[1], step[2])
            run_groups(dve, body)
            normalise(ngroups, ngroups * UNITS - 1, -1)
            ln_rows(ngroups * 8 - 1, 3, ngroups * UNITS - 1)

        @block.tensor
        def _(pe):
            def turn(no, src, ready, count):
                wait(pe, ready, count)
                wait(pe, s_turn_lo, no)
                for k in range(KT):
                    last = nc.tensor.transpose(ps_turn[:, k * P:(k + 1) * P], src[:, k * P:(k + 1) * P], ident[:, :])
                last.then_inc(s_turn, 1)

            def half_tile(g, t, part):
                kind, m = TILE_KIND[t]
                hi, lo = (eT_hi, eT_lo) if kind in ("ek", "ev") else (hT_hi, hT_lo)
                if part == 0:
                    wait(pe, s_evac[t % 2], g * (TILES // 2) + (PRO_TILES // 2 + t // 2))
                for k in range(2 * part, 2 * part + 2):
                    for a, c in (("hi", "hi"), ("hi", "lo"), ("lo", "hi")):
                        if kind in ("v", "ev"):
                            lhsT = (hi if a == "hi" else lo)[:, k, m * P:(m + 1) * P]
                            rhs = (w_hi if c == "hi" else w_lo)[kind][:, k, :]
                        else:
                            lhsT = (w_hi if a == "hi" else w_lo)[kind][:, k, m * P:(m + 1) * P]
                            rhs = (hi if c == "hi" else lo)[:, k, :]
                        last = nc.tensor.matmul(ps_tile[t % 2][:, :], lhsT, rhs, start=(k == 0 and a + c == "hihi"),
                                                stop=(k == KT - 1 and a == "lo"))
                if part == 1:
                    last.then_inc(s_tile, 1)

            pe.wait_ge(s_ident, 2)
            for b in range(GB):
                turn(b, (x_row if b < 2 else h_row)[b % 2], s_relu, b + 1)
            pe.wait_ge(s_turn_lo, GB)

            def first_tiles(kinds):
                for t in range(TILES - PRO_TILES, TILES):
                    if TILE_KIND[t] in kinds:
                        pe.wait_ge(s_wlo, {"q": 1, "k": 2, "v": 3}[TILE_KIND[t][0]])
                        half_tile(-1, t, 0)
                        half_tile(-1, t, 1)

            first_tiles([(w_, m) for w_ in ("q", "k") for m in range(KT)])
            pe.wait_ge(s_const, 48)
            pe.wait_ge(s_stage[0], 48)
            for m in range(KT):
                for k in range(KT):
                    last = nc.tensor.matmul(ps_av[0][:, m:m + 1], proj["q2"][:, k, m * P:(m + 1) * P],
                                            col[:, COL["b1"], k:k + 1], start=(k == 0), stop=(k == KT - 1))
            last.then_inc(s_matvec, 1)
            first_tiles([("v", 0), ("v", 1)])
            pe.wait_ge(s_stage[1], 48)
            for k in range(KT):
                last = nc.tensor.matmul(ps_av[1][:, :], col[:, COL["b1"], k:k + 1].broadcast_to([P, P]),
                                        proj["ek"][:, k, :], start=(k == 0), stop=(k == KT - 1))
            last.then_inc(s_matvec, 1)
            first_tiles([("v", 2), ("v", 3)])
            pe.wait_ge(s_wlo, 6)
            pe.wait_ge(s_bias, 2)
            pe.wait_ge(s_ones, 2)

            def transpose_probs(n, u):
                pe.wait_ge(s_exp, n + 1)
                wait(pe, s_pt_evac, n)
                for j in range(HU):
                    last = nc.tensor.transpose(ps_probT[:, j * P:(j + 1) * P], prob[u % 2][:, j * P:(j + 1) * P], ident[:, :])
                last.then_inc(s_pt, 1)

            def attend(g, n, u):
                layer, b, par = (u % UNITS) // 8, (u % 8) // 2, u % 2
                pe.wait_ge(s_pt_evac, n + 1)
                wait(pe, s_norm, n - 1)
                if layer == 0 and u % UNITS < 2:
                    wait_tile(pe, g - 1, TILE_OF[("v", 2)])
                    wait_tile(pe, g - 1, TILE_OF[("v", 3)])
                elif layer == 1 and par == 0:
                    wait_tile(pe, g, TILE_OF[("ev", b)])
                for j in range(HU):
                    last = nc.tensor.matmul(ps_av[par][:, j * HV:(j + 1) * HV], probT[:, j * P:(j + 1) * P],
                                            val[("v", "ev")[layer]][:, b, 2 * j + par, :], start=True, stop=True)
                last.then_inc(s_av, 1)

            def body(g, first, last):
                for step in steps_of_group(first, last):
                    if step[0] == "scores":
                        u = step[1]
                        layer, b, par = u // 8, (u % 8) // 2, u % 2
                        n = g * UNITS + u
                        if not (first and u < 2):
                            pe.wait_ge(s_shift, n - 1)
                        if layer == 0 and par == 0:
                            pe.wait_ge(s_mask, g * GB + (b + 1))
                        if layer == 0 and u == 0:
                            wait_tile(pe, g - 1, TILE_OF[("q", 3)])
                            wait_tile(pe, g - 1, TILE_OF[("k", 3)])
                        if layer == 1 and u == 8:
                            wait_tile(pe, g, TILE_OF[("ek", 3)])
                            wait_tile(pe, g, TILE_OF[("ek", 2)])
                        out = ps_scores[u % 2]
                        if layer == 0:
                            nc.tensor.matmul(out[:, :], mask[:, b, :], ident_b[:, :].unsqueeze(1).broadcast_to([P, HU, P]),
                                             start=True, stop=False)
                        q, k = (proj["q"], proj["k"]) if layer == 0 else (proj["q2"], proj["ek"])
                        half = slice(HD * par, HD * (par + 1))
                        for j in range(HU):
                            mm = nc.tensor.matmul(out[:, j * P:(j + 1) * P], q[half, j, b * P:(b + 1) * P],
                                                  k[half, j, b * P:(b + 1) * P], start=(layer == 1),
                                                  stop=(layer == 1 or j == HU - 1))
                        mm.then_inc(s_scores, 1)
                    elif step[0] == "pt":
                        transpose_probs(g * UNITS + step[1], step[1] % UNITS)
                    elif step[0] == "av":
                        attend(g, g * UNITS + step[1], step[1] % UNITS)
                    elif step[0] == "half":
                        t, part = step[1:]
                        if part == 0 and TILE_KIND[t][0] in ("ev", "ek", "q"):
                            kind, m = TILE_KIND[t]
                            turned = ("edge", m) if kind == "ev" else ("edge", 3) if kind == "ek" else ("h", 3)
                            pe.wait_ge(s_turn_lo, turn_no(g, *turned) + 1)
                        half_tile(g, t, part)
                    elif step[0] == "t_edge":
                        b = step[1]
                        turn(turn_no(g, "edge", b), row[b], s_apply, g * 8 + (b + 1))
                    elif step[0] == "t_h":
                        b = step[1]
                        turn(turn_no(g, "h", b), x_row[b % 2], s_relu, g * GB + (GB + b + 1))
                    elif step[0] == "t_next":
                        b = step[1]
                        turn(turn_no(g, "next", b), early.rows[:, b, :], s_early_rows[b], 16)
            run_groups(pe, body)
            transpose_probs(ngroups * UNITS - 1, UNITS - 1)
            attend(ngroups - 1, ngroups * UNITS - 1, UNITS - 1)


def ffn_steps(g_first, g_last, prep):
    out = []
    for t in range(FT):
        out.extend([("up", t), ("gelu", t)])
        if g_first and t >= FT - 2:
            out.extend([("turn", b) for b in range(GB) if b // 2 == t - (FT - 2)])
        if prep and t + 2 < FT:
            out.extend([("prep", t + 2)])
        if t or not g_first:
            out.append(("down", t - 1))
        out.append(("split", t))
        if t == 0 and not g_first:
            out.extend([("add_res", mt) for mt in range(GB)])
        if 1 <= t <= GB and not g_first:
            out.append(("finish", t - 1))
        if 2 <= t <= GB + 1 and not g_first:
            out.append(("gain", t - 2))
        if 5 <= t < 5 + GB and not g_last and not g_first:
            out.append(("load_n2", t - 5))
        if 7 <= t < 7 + GB:
            out.append(("load_x", t - 7))
        if 11 <= t < 11 + GB:
            out.append(("shift_x", t - 11))
        if t >= FT - 3 and g_first and t < FT - 1:
            out.extend([("load_n2", b) for b in range(2 * (t - FT + 3), 2 * (t - FT + 3) + 2)])
        if not (g_first or g_last) and t in (8, 10, 12, 14):
            out.append(("turn", t // 2 - 4))
    return out


def ffn_pass(nc, early, n2, x, w1, w2, rows_in, out):
    ident, neg_half, col, bias_up, stage1, stage2 = (early.ident, early.neg_half, early.col, early.bias_up,
                                                     early.stage1, early.stage2)
    ngroups = x.shape[0] // GB
    x_v = x.rearrange("(g b) p d -> g b p d", b=GB)
    n2_v = n2.rearrange("(g b) p d -> g b p d", b=GB)
    out_v = out.rearrange("(g b) p d -> g b p d", b=GB)
    w1_v, w2_v = w1_tiles(w1), w2_tiles(w2)

    def graph(view, g, b):
        if isinstance(g, int):
            return view[g, b]
        return view[bass.ds(g, 1), b].rearrange("o p d -> (o p) d")

    ctx = ExitStack()
    with ctx:
        def sb(name, shape, dt=F32):
            return ctx.enter_context(nc.sbuf_tensor(name, shape, dt))

        def sem(name):
            return ctx.enter_context(nc.semaphore(name))

        w1_hi, w1_lo = sb("w1_hi", [P, KT, DF], F32R), sb("w1_lo", [P, KT, DF], F32R)
        w2_hi, w2_lo = sb("w2_hi", [P, FT, D], F32R), sb("w2_lo", [P, FT, D], F32R)
        nT_hi = [early.nT_hi, sb("nT_hi1", [P, KT, R], F32R)]
        nT_lo = [early.nT_lo, sb("nT_lo1", [P, KT, R], F32R)]
        n_row = [early.rows, early.stage]
        x_res = [sb(f"x_res{i}", [P, D]) for i in range(GB)]
        act_f = [sb(f"act_f{i}", [P, R]) for i in range(2)]
        act_hi = [sb(f"act_hi{i}", [P, R], F32R) for i in range(2)]
        act_lo = [sb(f"act_lo{i}", [P, R], F32R) for i in range(2)]
        gain2, shift2 = sb("gain2", [P, D]), sb("shift2", [P, D])
        gain3, shift3 = sb("gain3", [P, D]), sb("shift3", [P, D])
        turned = sb("turned", [P, D])
        bias_down = act_f[1]
        st = sb("fst", [P, 2, 6])
        mv = sb("fmv", [P, 2, 2])
        var = sb("fvar", [P, 1])
        ln = sb("fln", [P, 2, 2])

        bank = [ctx.enter_context(nc.psum_tensor(f"fbank{i}", [P, 512], F32)) for i in range(8)]
        ps_up, ps_down, ps_turn = bank[0:2], bank[2:6], bank[6:8]

        s_rows = sem("f_rows")
        s_shift2 = sem("f_shift2")
        s_w1in = [sem(f"f_w1in{i}") for i in range(2)]
        s_w2in = [sem(f"f_w2in{i}") for i in range(2)]
        s_whi, s_wlo = sem("f_whi"), sem("f_wlo")
        s_n2in = [sem(f"f_n2in{b}") for b in range(GB)]
        s_xin = [sem(f"f_xin{i}") for i in range(GB)]
        s_turn, s_turned, s_turn_hi, s_turn_lo = sem("f_turn"), sem("f_turned"), sem("f_turn_hi"), sem("f_turn_lo")
        s_gain, s_res = sem("f_gain"), sem("f_res")
        s_up, s_gelu, s_act_hi, s_act = sem("f_up"), sem("f_gelu"), sem("f_act_hi"), sem("f_act")
        s_down = sem("f_down")
        s_sum = sem("f_sum")
        s_bn, s_mv, s_var, s_rstd, s_ln = (sem(f"f_{n}") for n in ("bn", "mv", "var", "rstd", "ln"))
        s_apply, s_gain3, s_xb, s_out = sem("f_apply"), sem("f_gain3"), sem("f_xb"), sem("f_out")
        s_store = [sem(f"f_store{b}") for b in range(GB)]

        def run_pairs(eng, body):
            body(0, 0, True, False)
            body(1, 1, False, False)
            with eng.Fori(1, ngroups // 2 - 1) as pair:
                body(pair * 2, 0, False, False)
                body(pair * 2 + 1, 1, False, False)
            body(ngroups - 2, 0, False, False)
            body(ngroups - 1, 1, False, True)

        block = ctx.enter_context(nc.Block())

        @block.sync
        def _(sp):
            def load_n2(g, par, b):
                sp.dma_start(n_row[par][:, b, :], graph(n2_v, g, b)).then_inc(s_n2in[b], 16)

            def load_x(g, b):
                sp.dma_start(x_res[b][:, :], graph(x_v, g, b)).then_inc(s_xin[b], 16)

            def load_weights(t):
                sp.wait_ge(s_wlo, 2 * (t - 1))
                sp.dma_start(stage1[t % 2], w1_v[t]).then_inc(s_w1in[t % 2], 16)
                sp.dma_start(stage2[t % 2], w2_v[t]).then_inc(s_w2in[t % 2], 16)

            def store(g, par, b):
                wait_alone(sp, s_out, g * GB + (b + 1))
                sp.dma_start(graph(out_v, g, b), n_row[par][:, b, :]).then_inc(s_store[b], 16)

            for dst, src in zip((gain2[:, :], shift2[:, :], bias_down[:, :], gain3[:, :], shift3[:, :]), rows_in):
                sp.dma_start(dst, src.partition_broadcast(P)).then_inc(s_rows, 16)

            def body(g, par, first, last):
                for step in ffn_steps(first, last, first):
                    if step[0] == "prep":
                        load_weights(step[1])
                    elif step[0] == "load_n2":
                        b = step[1]
                        if first:
                            sp.wait_ge(s_wlo, 2 * (FT - 1 + b // 2))
                        else:
                            wait_alone(sp, s_store[b], g * 16)
                        load_n2(g + 1, 1 - par, b)
                    elif step[0] == "load_x":
                        wait_alone(sp, s_out, g * GB + (step[1] + 1 - GB))
                        load_x(g, step[1])
                    elif step[0] == "gain":
                        store(g - 1, 1 - par, step[1])
            run_pairs(sp, body)
            for b in range(GB):
                store(ngroups - 1, 1, b)
            for b in range(GB):
                sp.wait_ge(s_store[b], 16 * ngroups)

        @block.gpsimd
        def _(pool):
            pool.wait_ge(s_rows, 16 * 5)
            nc.gpsimd.tensor_tensor(shift2[:, :], shift2[:, :], bias_down[:, :], ALU.add).then_inc(s_shift2, 1)
            pool.wait_ge(s_shift2, 1)

            def residual(n, par, b):
                if not (isinstance(n, int) and n < GB):
                    pool.wait_ge(s_turn, n + (1 - GB))
                nc.gpsimd.tensor_tensor(n_row[par][:, b, :], n_row[par][:, b, :], gain2[:, :], ALU.mult).then_inc(s_gain, 1)
                pool.wait_ge(s_gain, n + 1)
                nc.gpsimd.tensor_tensor(n_row[par][:, b, :], n_row[par][:, b, :], shift2[:, :], ALU.add).then_inc(s_res, 1)

            def finish(g, par, b):
                n = g * GB + b
                wait_alone(pool, s_mv, n + 1)
                nc.gpsimd.tensor_scalar(var[:, :], mv[:, b % 2, 1:2], LN_EPS, None, ALU.add).then_inc(s_var, 1)
                pool.wait_ge(s_var, n + 1)
                if not (isinstance(g, int) and n < 2):
                    pool.wait_ge(s_apply, n - 1)
                nc.gpsimd.tensor_tensor(ln[:, b % 2, 0:1], var[:, :], neg_half[:, :], ALU.pow).then_inc(s_rstd, 1)
                wait_alone(pool, s_rstd, n + 1)
                nc.gpsimd.tensor_scalar(ln[:, b % 2, 1:2], mv[:, b % 2, 0:1], ln[:, b % 2, 0:1], -1.0,
                                        ALU.mult, ALU.mult).then_inc(s_ln, 1)

            def shift_x(g, b):
                pool.wait_ge(s_xin[b], g * 16 + 16)
                nc.gpsimd.tensor_tensor(x_res[b][:, :], x_res[b][:, :], shift3[:, :], ALU.add).then_inc(s_xb, 1)

            def add_x(g, par, b):
                n = g * GB + b
                pool.wait_ge(s_gain3, n + 1)
                pool.wait_ge(s_xb, n + 1)
                nc.gpsimd.tensor_tensor(n_row[par][:, b, :], n_row[par][:, b, :], x_res[b][:, :], ALU.add).then_inc(s_out, 1)

            for b in range(GB):
                residual(b, 0, b)

            def body(g, par, first, last):
                for step in ffn_steps(first, last, first):
                    if step[0] == "turn":
                        residual(g * GB + (GB + step[1]), 1 - par, step[1])
                    elif step[0] == "finish":
                        finish(g - 1, 1 - par, step[1])
                    elif step[0] == "gain":
                        add_x(g - 1, 1 - par, step[1])
                    elif step[0] == "shift_x":
                        shift_x(g, step[1])
            run_pairs(pool, body)
            for b in range(GB):
                finish(ngroups - 1, 1, b)
                if b:
                    add_x(ngroups - 1, 1, b - 1)
            add_x(ngroups - 1, 1, GB - 1)

        @block.scalar
        def _(act):
            def turn_norm(n, b):
                act.wait_ge(s_turn, n + 1)
                wait(act, s_turn_lo, n)
                for k in range(KT):
                    sl = slice(k * P, (k + 1) * P)
                    last = nc.scalar.activation(turned[:, sl], ps_turn[b % 2][:, sl], ACT.Identity,
                                                bias=col[:, 1, k:k + 1], scale=col[:, 0, k:k + 1])
                last.then_inc(s_turned, 1)

            def prep_hi(t):
                wait(act, s_w1in[t % 2], 16 * (t // 2))
                nc.scalar.activation(w1_hi[:, :, t * P:(t + 1) * P], stage1[t % 2], ACT.Copy).then_inc(s_whi, 1)
                wait(act, s_w2in[t % 2], 16 * (t // 2))
                nc.scalar.activation(w2_hi[:, t, :], stage2[t % 2], ACT.Copy).then_inc(s_whi, 1)

            def apply(n, par, b):
                act.wait_ge(s_ln, n + 1)
                nc.scalar.activation(n_row[par][:, b, :], n_row[par][:, b, :], ACT.Identity, bias=ln[:, b % 2, 1:2],
                                     scale=ln[:, b % 2, 0:1]).then_inc(s_apply, 1)

            prep_hi(0)
            prep_hi(1)

            def body(g, par, first, last):
                for step in ffn_steps(first, last, first):
                    if step[0] == "gelu":
                        t = step[1]
                        n = g * FT + t
                        act.wait_ge(s_up, n + 1)
                        if first and t < 2:
                            act.wait_ge(s_shift2, 1)
                        else:
                            act.wait_ge(s_act, n - 1)
                        nc.scalar.activation(act_f[t % 2][:, :], ps_up[t % 2][:, :], ACT.Gelu,
                                             bias=bias_up[:, t:t + 1]).then_inc(s_gelu, 1)
                    elif step[0] == "prep":
                        prep_hi(step[1])
                    elif step[0] == "turn":
                        turn_norm(g * GB + step[1], step[1])
                    elif step[0] == "finish":
                        apply(g * GB + (step[1] - GB), 1 - par, step[1])
            run_pairs(act, body)
            for b in range(GB):
                apply((ngroups - 1) * GB + b, 1, b)

        @block.vector
        def _(dve):
            def turn_split(n, par, b):
                src = turned[:, :].rearrange("p (k r) -> p k r", k=KT)
                hi = nT_hi[par][:, :, b * P:(b + 1) * P]
                dve.wait_ge(s_turned, n + 1)
                nc.vector.tensor_copy(hi, src).then_inc(s_turn_hi, 1)
                dve.wait_ge(s_turn_hi, n + 1)
                nc.vector.tensor_tensor(nT_lo[par][:, :, b * P:(b + 1) * P], src, hi.bitcast(F32),
                                        ALU.subtract).then_inc(s_turn_lo, 1)

            def prep(t):
                dve.wait_ge(s_whi, 2 * t + 1)
                nc.vector.tensor_tensor(w1_lo[:, :, t * P:(t + 1) * P], stage1[t % 2],
                                        w1_hi[:, :, t * P:(t + 1) * P].bitcast(F32), ALU.subtract).then_inc(s_wlo, 1)
                dve.wait_ge(s_whi, 2 * t + 2)
                nc.vector.tensor_tensor(w2_lo[:, t, :], stage2[t % 2], w2_hi[:, t, :].bitcast(F32),
                                        ALU.subtract).then_inc(s_wlo, 1)

            def stats(g, n, par, b):
                if not (isinstance(n, int) and n < 2):
                    dve.wait_ge(s_ln, n - 1)
                dve.wait_ge(s_sum, n + 1)
                nc.vector.bn_stats(st[:, b % 2, :], n_row[par][:, b, :]).then_inc(s_bn, 1)
                wait_alone(dve, s_bn, n + 1)
                nc.vector.bn_aggr(mv[:, b % 2, :], st[:, b % 2, :]).then_inc(s_mv, 1)

            def add_residual(g, par, b):
                n = g * GB + b
                dve.wait_ge(s_down, g * (FT * GB) + ((FT - 1) * GB + b + 1))
                dve.wait_ge(s_res, n + 1)
                nc.vector.tensor_tensor(n_row[par][:, b, :], ps_down[b][:, :], n_row[par][:, b, :], ALU.add).then_inc(s_sum, 1)

            def gain(n, par, b):
                dve.wait_ge(s_apply, n + 1)
                nc.vector.tensor_tensor(n_row[par][:, b, :], n_row[par][:, b, :], gain3[:, :], ALU.mult).then_inc(s_gain3, 1)

            prep(0)
            prep(1)

            def body(g, par, first, last):
                for step in ffn_steps(first, last, first):
                    if step[0] == "split":
                        t = step[1]
                        n = g * FT + t
                        dve.wait_ge(s_gelu, n + 1)
                        if not (first and t < 2):
                            dve.wait_ge(s_down, g * (FT * GB) + (t - 1) * GB)
                        nc.vector.tensor_copy(act_hi[t % 2][:, :], act_f[t % 2][:, :]).then_inc(s_act_hi, 1)
                        dve.wait_ge(s_act_hi, n + 1)
                        nc.vector.tensor_tensor(act_lo[t % 2][:, :], act_f[t % 2][:, :], act_hi[t % 2][:, :].bitcast(F32),
                                                ALU.subtract).then_inc(s_act, 1)
                    elif step[0] == "prep":
                        prep(step[1])
                    elif step[0] == "add_res":
                        add_residual(g - 1, 1 - par, step[1])
                    elif step[0] == "finish":
                        stats(g - 1, g * GB + (step[1] - GB), 1 - par, step[1])
                    elif step[0] == "gain":
                        gain(g * GB + (step[1] - GB), 1 - par, step[1])
                    elif step[0] == "turn":
                        turn_split(g * GB + step[1], 1 - par, step[1])
                if first:
                    dve.wait_ge(s_rows, 16 * 5)
            run_pairs(dve, body)
            for b in range(GB):
                add_residual(ngroups - 1, 1, b)
                stats(ngroups - 1, (ngroups - 1) * GB + b, 1, b)
                if b:
                    gain((ngroups - 1) * GB + b - 1, 1, b - 1)
            gain(ngroups * GB - 1, 1, GB - 1)

        @block.tensor
        def _(pe):
            def turn(n, g, par, b):
                pe.wait_ge(s_n2in[b], g * 16 + 16)
                wait(pe, s_turned, n - 1)
                for k in range(KT):
                    last = nc.tensor.transpose(ps_turn[b % 2][:, k * P:(k + 1) * P], n_row[par][:, b, k * P:(k + 1) * P], ident[:, :])
                last.then_inc(s_turn, 1)

            def down(g, t, first_group):
                pe.wait_ge(s_act, g * FT + (t + 1))
                if first_group:
                    pe.wait_ge(s_wlo, 2 * (t + 1))
                for b in range(GB):
                    if t == 0 and not first_group:
                        pe.wait_ge(s_sum, g * GB + (b + 1 - GB))
                    sl = slice(b * P, (b + 1) * P)
                    for i, (a, c) in enumerate(((act_hi, w2_hi), (act_hi, w2_lo), (act_lo, w2_hi))):
                        mm = nc.tensor.matmul(ps_down[b][:, :], a[t % 2][:, sl], c[:, t, :], start=(t == 0 and i == 0),
                                              stop=(t == FT - 1 and i == 2))
                    mm.then_inc(s_down, 1)

            def body(g, par, first, last):
                for step in ffn_steps(first, last, first):
                    if step[0] == "up":
                        t = step[1]
                        n = g * FT + t
                        if not (first and t < 2):
                            pe.wait_ge(s_gelu, n - 1)
                        if t == 0:
                            wait(pe, s_turn_lo, g * GB)
                        if first:
                            pe.wait_ge(s_wlo, 2 * t + 1)
                        for k in range(KT):
                            for i, (a, c) in enumerate(((w1_hi, nT_hi), (w1_hi, nT_lo), (w1_lo, nT_hi))):
                                mm = nc.tensor.matmul(ps_up[t % 2][:, :], a[:, k, t * P:(t + 1) * P], c[par][:, k, :],
                                                      start=(k == 0 and i == 0), stop=(k == KT - 1 and i == 2))
                        mm.then_inc(s_up, 1)
                    elif step[0] == "down":
                        if step[1] < 0:
                            down(g - 1, FT - 1, False)
                        else:
                            down(g, step[1], first)
                    elif step[0] == "turn":
                        turn(g * GB + step[1], g, 1 - par, step[1])
            run_pairs(pe, body)
            down(ngroups - 1, FT - 1, False)


def kernel(**inputs):
    import numpy as np
    import concourse.bacc as _bacc
    from concourse import mybir as _mybir
    from concourse.bass_utils import run_bass_kernel_spmd as _run

    pre = "L0_gnn_"

    def col(name):
        return np.asarray(inputs[pre + name]).reshape(-1, P).T

    arrays = {"x": np.ascontiguousarray(inputs["x"]), "adj": np.ascontiguousarray(inputs["adj"])}
    weights = (("q", "n2e_q"), ("k", "n2e_k"), ("v", "n2e_v"), ("q2", "e2n_q"), ("ek", "e2n_k"), ("ev", "e2n_v"))
    for short, name in weights:
        arrays[f"w_{short}"] = np.ascontiguousarray(np.asarray(inputs[f"{pre}{name}_w"]).T)
    for short in ("ffn_w1", "ffn_w2"):
        arrays[short] = np.ascontiguousarray(np.asarray(inputs[pre + short]).T)
    arrays["cols"] = np.ascontiguousarray(np.stack([col(n) for n in (
        "n2e_q_b", "n2e_k_b", "e2n_q_b", "e2n_k_b", "norm1_g", "norm1_b")], axis=1))
    arrays["cols_norm2"] = np.ascontiguousarray(np.stack([col("norm2_g"), col("norm2_b")], axis=1))
    arrays["cols_ffn_b1"] = np.ascontiguousarray(col("ffn_b1"))
    rows = ("n2e_v_b", "e2n_v_b", "norm2_g", "norm2_b", "ffn_b2", "norm3_g", "norm3_b")
    for name in rows:
        arrays[name] = np.ascontiguousarray(inputs[pre + name])
    nc = _bacc.Bacc("TRN2", target_bir_lowering=False, num_devices=1)
    ap = {n: nc.dram_tensor(f"in_{n}", a.shape, _mybir.dt.from_np(a.dtype), kind="ExternalInput").ap()
          for n, a in arrays.items()}
    shape = tuple(inputs["x"].shape)
    n2 = nc.dram_tensor("n2_scratch", shape, _mybir.dt.float32, kind="Internal").ap()
    out = nc.dram_tensor("out_0", shape, _mybir.dt.float32, kind="ExternalOutput").ap()
    with ExitStack() as ctx:
        early = Early(nc, ctx)
        attention_pass(nc, early, ap["x"], ap["adj"], {k: ap[f"w_{k}"] for k, _ in weights}, ap["cols"],
                       tuple(ap[n] for n in rows[:2]), n2, ap["ffn_w1"], ap["ffn_w2"],
                       (ap["cols_norm2"], ap["cols_ffn_b1"]))
        ffn_pass(nc, early, n2, ap["x"], ap["ffn_w1"], ap["ffn_w2"], tuple(ap[n] for n in rows[2:]), out)
    r = _run(nc, [{f"in_{n}": a for n, a in arrays.items()}], core_ids=[0])
    return r.results[0]["out_0"]
```
